# Optimizing a Trainium2 kernel written in Bass

```python
import numpy as np
import jax
import jax.numpy as jnp

def _softmax(x, axis=-1):
    return jax.nn.softmax(x, axis=axis)

def _gelu(x):
    return jax.nn.gelu(x, approximate=True)

def _silu(x):
    return jax.nn.silu(x)

def _sigmoid(x):
    return jax.nn.sigmoid(x)

def _layernorm(x, axis=-1, eps=1e-05):
    m = jnp.mean(x, axis=axis, keepdims=True)
    v = jnp.var(x, axis=axis, keepdims=True)
    return (x - m) / jnp.sqrt(v + eps)

def _scatter_add(tgt, idx, src, axis=0):
    return tgt.at[idx].add(src)

def _segment_sum(src, seg, n):
    return jax.ops.segment_sum(src, seg, n)
kernel_name = 'mk_macaron_d1_jaxref_r8_d026f2'

def setup_inputs(seed: int=0):
    np.random.seed(seed)
    _w = jnp.asarray

    def _L0_attn_setup():
        import jax, jax.numpy as jnp
        import numpy as np
        NUM_HEADS = 16
        HIDDEN = 128
        HEAD_DIM = HIDDEN // NUM_HEADS
        B, L = (1, 256)
        key = jax.random.key(seed)
        ks = jax.random.split(key, 5)
        scale = 1.0 / np.sqrt(HIDDEN)
        x = jax.random.normal(ks[0], (B, L, HIDDEN), dtype=jnp.float32)
        Wq = jax.random.normal(ks[1], (HIDDEN, HIDDEN), dtype=jnp.float32) * scale
        Wk = jax.random.normal(ks[2], (HIDDEN, HIDDEN), dtype=jnp.float32) * scale
        Wv = jax.random.normal(ks[3], (HIDDEN, HIDDEN), dtype=jnp.float32) * scale
        Wo = jax.random.normal(ks[4], (HIDDEN, HIDDEN), dtype=jnp.float32) * scale
        return {'x': x, 'Wq': Wq, 'Wk': Wk, 'Wv': Wv, 'Wo': Wo}
    _L0_attn_in = _L0_attn_setup()

    def _L0_ffn_setup():
        import jax, jax.numpy as jnp
        import numpy as np
        EMB = 128
        HID = 256
        HEADS = 16
        HEAD_DIM = EMB // HEADS
        EXPERTS = 8
        TOPK = 2
        EPS = 1e-05

        def layernorm(x, scale, shift):
            mean = jnp.mean(x, axis=-1, keepdims=True)
            var = jnp.mean((x - mean) ** 2, axis=-1, keepdims=True)
            return scale * (x - mean) / jnp.sqrt(var + EPS) + shift

        def attention(x, wq, wk, wv, wo, bo):
            b, t, _ = x.shape
            q = (x @ wq).reshape(b, t, HEADS, HEAD_DIM)
            k = (x @ wk).reshape(b, t, HEADS, HEAD_DIM)
            v = (x @ wv).reshape(b, t, HEADS, HEAD_DIM)
            scores = jnp.einsum('bqhd,bkhd->bhqk', q, k)
            mask = jnp.arange(t)[:, None] < jnp.arange(t)[None, :]
            scores = jnp.where(mask, -jnp.inf, scores)
            attn = jax.nn.softmax(scores / np.sqrt(HEAD_DIM), axis=-1)
            ctx = jnp.einsum('bhqk,bkhd->bqhd', attn, v).reshape(b, t, EMB)
            return ctx @ wo + bo

        def moe_ff(x, gate_w, w1, w2, w3):
            b, t, d = x.shape
            xf = x.reshape(b * t, d)
            scores = xf @ gate_w
            topk_scores, topk_idx = jax.lax.top_k(scores, TOPK)
            topk_probs = jax.nn.softmax(topk_scores, axis=-1)
            weight = jnp.sum(jax.nn.one_hot(topk_idx, EXPERTS, dtype=xf.dtype) * topk_probs[..., None], axis=1)
            h = jax.nn.silu(jnp.einsum('td,edh->eth', xf, w1)) * jnp.einsum('td,edh->eth', xf, w2)
            out_e = jnp.einsum('eth,ehd->etd', h, w3)
            out = jnp.einsum('etd,te->td', out_e, weight)
            return out.reshape(b, t, d)
        key = jax.random.key(seed)
        ks = jax.random.split(key, 12)
        s = lambda k, shape, fan: jax.random.normal(k, shape, jnp.float32) / np.sqrt(fan)
        return {'x': jax.random.normal(ks[0], (2, 256, EMB), jnp.float32), 'ln1_scale': jnp.ones((EMB,), jnp.float32), 'ln1_shift': jnp.zeros((EMB,), jnp.float32), 'wq': s(ks[1], (EMB, EMB), EMB), 'wk': s(ks[2], (EMB, EMB), EMB), 'wv': s(ks[3], (EMB, EMB), EMB), 'wo': s(ks[4], (EMB, EMB), EMB), 'bo': jnp.zeros((EMB,), jnp.float32), 'ln2_scale': jnp.ones((EMB,), jnp.float32), 'ln2_shift': jnp.zeros((EMB,), jnp.float32), 'gate_w': s(ks[5], (EMB, EXPERTS), EMB), 'w1': s(ks[6], (EXPERTS, EMB, HID), EMB), 'w2': s(ks[7], (EXPERTS, EMB, HID), EMB), 'w3': s(ks[8], (EXPERTS, HID, EMB), HID)}
    _L0_ffn_in = _L0_ffn_setup()
    _d = {'L0_attn_x': _L0_attn_in['x'], 'L0_attn_Wq': _L0_attn_in['Wq'], 'L0_attn_Wk': _L0_attn_in['Wk'], 'L0_attn_Wv': _L0_attn_in['Wv'], 'L0_attn_Wo': _L0_attn_in['Wo'], 'L0_ffn_ln1_scale': _L0_ffn_in['ln1_scale'], 'L0_ffn_ln1_shift': _L0_ffn_in['ln1_shift'], 'L0_ffn_wq': _L0_ffn_in['wq'], 'L0_ffn_wk': _L0_ffn_in['wk'], 'L0_ffn_wv': _L0_ffn_in['wv'], 'L0_ffn_wo': _L0_ffn_in['wo'], 'L0_ffn_bo': _L0_ffn_in['bo'], 'L0_ffn_ln2_scale': _L0_ffn_in['ln2_scale'], 'L0_ffn_ln2_shift': _L0_ffn_in['ln2_shift'], 'L0_ffn_gate_w': _L0_ffn_in['gate_w'], 'L0_ffn_w1': _L0_ffn_in['w1'], 'L0_ffn_w2': _L0_ffn_in['w2'], 'L0_ffn_w3': _L0_ffn_in['w3']}
    _x0 = _d['L0_attn_x']
    _d['L0_attn_x'] = jax.random.normal(jax.random.fold_in(jax.random.key(seed), 1), (16, 256, 128), dtype=_x0.dtype)
    del _x0
    return _d

def reference(L0_attn_x, L0_attn_Wq, L0_attn_Wk, L0_attn_Wv, L0_attn_Wo, L0_ffn_ln1_scale, L0_ffn_ln1_shift, L0_ffn_wq, L0_ffn_wk, L0_ffn_wv, L0_ffn_wo, L0_ffn_bo, L0_ffn_ln2_scale, L0_ffn_ln2_shift, L0_ffn_gate_w, L0_ffn_w1, L0_ffn_w2, L0_ffn_w3):

    def _L0_attn_ref(x, Wq, Wk, Wv, Wo):
        import jax, jax.numpy as jnp
        import numpy as np
        NUM_HEADS = 16
        HIDDEN = 128
        HEAD_DIM = HIDDEN // NUM_HEADS
        B, L = (1, 256)
        Bx, Lx, _ = x.shape
        q = (x @ Wq.T).reshape(Bx, Lx, NUM_HEADS, HEAD_DIM)
        k = (x @ Wk.T).reshape(Bx, Lx, NUM_HEADS, HEAD_DIM)
        v = (x @ Wv.T).reshape(Bx, Lx, NUM_HEADS, HEAD_DIM)
        q = jax.nn.elu(q) + 1.0
        k = jax.nn.elu(k) + 1.0
        kv = jnp.einsum('blhd,blhe->blhde', k, v)
        kv_cumsum = jnp.cumsum(kv, axis=1)
        k_cumsum = jnp.cumsum(k, axis=1)
        out = jnp.einsum('blhd,blhde->blhe', q, kv_cumsum)
        denom = jnp.clip(jnp.einsum('blhd,blhd->blh', q, k_cumsum), 1e-06, None)
        out = out / denom[..., None]
        return out.reshape(Bx, Lx, HIDDEN) @ Wo.T

    def _L0_ffn_ref(x, ln1_scale, ln1_shift, wq, wk, wv, wo, bo, ln2_scale, ln2_shift, gate_w, w1, w2, w3):
        import jax, jax.numpy as jnp
        import numpy as np
        EMB = 128
        HID = 256
        HEADS = 16
        HEAD_DIM = EMB // HEADS
        EXPERTS = 8
        TOPK = 2
        EPS = 1e-05

        def layernorm(x, scale, shift):
            mean = jnp.mean(x, axis=-1, keepdims=True)
            var = jnp.mean((x - mean) ** 2, axis=-1, keepdims=True)
            return scale * (x - mean) / jnp.sqrt(var + EPS) + shift

        def attention(x, wq, wk, wv, wo, bo):
            b, t, _ = x.shape
            q = (x @ wq).reshape(b, t, HEADS, HEAD_DIM)
            k = (x @ wk).reshape(b, t, HEADS, HEAD_DIM)
            v = (x @ wv).reshape(b, t, HEADS, HEAD_DIM)
            scores = jnp.einsum('bqhd,bkhd->bhqk', q, k)
            mask = jnp.arange(t)[:, None] < jnp.arange(t)[None, :]
            scores = jnp.where(mask, -jnp.inf, scores)
            attn = jax.nn.softmax(scores / np.sqrt(HEAD_DIM), axis=-1)
            ctx = jnp.einsum('bhqk,bkhd->bqhd', attn, v).reshape(b, t, EMB)
            return ctx @ wo + bo

        def moe_ff(x, gate_w, w1, w2, w3):
            b, t, d = x.shape
            xf = x.reshape(b * t, d)
            scores = xf @ gate_w
            topk_scores, topk_idx = jax.lax.top_k(scores, TOPK)
            topk_probs = jax.nn.softmax(topk_scores, axis=-1)
            weight = jnp.sum(jax.nn.one_hot(topk_idx, EXPERTS, dtype=xf.dtype) * topk_probs[..., None], axis=1)
            h = jax.nn.silu(jnp.einsum('td,edh->eth', xf, w1)) * jnp.einsum('td,edh->eth', xf, w2)
            out_e = jnp.einsum('eth,ehd->etd', h, w3)
            out = jnp.einsum('etd,te->td', out_e, weight)
            return out.reshape(b, t, d)
        h = layernorm(x, ln1_scale, ln1_shift)
        x = x + attention(h, wq, wk, wv, wo, bo)
        h = layernorm(x, ln2_scale, ln2_shift)
        x = x + moe_ff(h, gate_w, w1, w2, w3)
        return x
    x = L0_attn_x
    x = x + 0.5 * _L0_ffn_ref(_layernorm(x, axis=-1), L0_ffn_ln1_scale, L0_ffn_ln1_shift, L0_ffn_wq, L0_ffn_wk, L0_ffn_wv, L0_ffn_wo, L0_ffn_bo, L0_ffn_ln2_scale, L0_ffn_ln2_shift, L0_ffn_gate_w, L0_ffn_w1, L0_ffn_w2, L0_ffn_w3)
    x = x + _L0_attn_ref(_layernorm(x, axis=-1), L0_attn_Wq, L0_attn_Wk, L0_attn_Wv, L0_attn_Wo)
    x = x + 0.5 * _L0_ffn_ref(_layernorm(x, axis=-1), L0_ffn_ln1_scale, L0_ffn_ln1_shift, L0_ffn_wq, L0_ffn_wk, L0_ffn_wv, L0_ffn_wo, L0_ffn_bo, L0_ffn_ln2_scale, L0_ffn_ln2_shift, L0_ffn_gate_w, L0_ffn_w1, L0_ffn_w2, L0_ffn_w3)
    return x

_drawn_inputs = setup_inputs


def setup_inputs(seed=0):
    import zlib

    import numpy as np

    out = dict(_drawn_inputs(seed))
    spreads = {'L0_ffn_ln1_scale': (1.0, 0.2),
     'L0_ffn_ln1_shift': (0.0, 0.1),
     'L0_ffn_bo': (0.0, 0.1),
     'L0_ffn_ln2_scale': (1.0, 0.2),
     'L0_ffn_ln2_shift': (0.0, 0.1)}
    factors = {'L0_attn_Wq': 3.031}
    for name, (base, spread) in spreads.items():
        noise = np.random.default_rng([zlib.crc32(name.encode()), seed]).standard_normal(out[name].shape)
        drawn = base * np.exp(spread * noise) if base else spread * noise
        out[name] = jnp.asarray(drawn.astype(out[name].dtype))
    for name, factor in factors.items():
        out[name] = (out[name] * factor).astype(out[name].dtype)
    return out
```

```python
from contextlib import ExitStack

import concourse.bass as bass
from concourse import mybir

F32 = mybir.dt.float32
F16 = mybir.dt.float16
BF16 = mybir.dt.bfloat16
U32 = mybir.dt.uint32
ALU = mybir.AluOpType
ACT = mybir.ActivationFunctionType
AX = mybir.AxisListType

P = 128
B = 16
T = 2
NT = B * T
H = 16
HD = P // H
G = 4
S = H // 2
VC = 2 * HD + 1
E = 8
HID = 256
HC = HID // P
CH = 4
EPS = 1e-5
BIG = -1e30
FRONT_V = 2


class Chain:

    def __init__(self, eng, sem, base):
        self.eng, self.sem, self.base, self.n = eng, sem, base, 0

    def link(self, ins):
        ins.then_inc(self.sem, 1)
        self.n += 1
        self.eng.wait_ge(self.sem, self.base + self.n)

    def end(self, n):
        assert self.n == n, (self.n, n)


def tile_at(array, b):
    return array[:, b, :, :]


def build(nc, x, Wq, Wk, Wv, Wo, ln1_s, ln1_b, wq, wk, wv, wo, bo, ln2_s, ln2_b, gate_w, w1, w2, w3, out):
    ctx = ExitStack()

    def sb(name, shape, dt=F32):
        return ctx.enter_context(nc.sbuf_tensor(name, shape, dt))

    with ctx:
        x_all = sb("x_all", [P, B, T, P])
        y_all = sb("y_all", [P, B, T, P])
        h2t_all = sb("h2t_all", [P, NT, P])
        gates = sb("gates", [P, NT, E])
        route = sb("route", [P, NT, E])
        top = sb("top", [P, NT, 8])
        topi = sb("topi", [P, NT, 8], U32)
        topf = sb("topf", [P, NT, 2])
        prob = sb("prob", [P, NT, 3])
        onehot = sb("onehot", [P, NT, E])
        w_qk = [sb(f"w_qk{n}", [P, 2, P]) for n in range(2)]
        w_v = [sb(f"w_v{n}", [P, P]) for n in range(2)]
        w_o = [sb(f"w_o{n}", [P, P]) for n in range(2)]
        ln = sb("ln", [P, 4])
        bo_b = sb("bo_b", [P, P])
        gw = sb("gw", [P, E])
        w12 = sb("w12", [P, E, 2, HID])
        w3s = sb("w3s", [P, E, HC, P])
        ident = sb("ident", [P, P])
        ident16 = sb("ident16", [P, P], F16)
        identb = sb("identb", [P, P], BF16)
        maskb = sb("maskb", [P, 2, P], BF16)
        sel = sb("sel", [P, 2, 2, G, 4, 4, HD], F16)
        iota_e = sb("iota_e", [P, E])
        half = sb("half", [P, T])
        st = sb("st", [P, T, 6])
        mv = sb("mv", [P, T, 2])
        rs = sb("rs", [P, 6, T])
        st2 = sb("st2", [P, T, 6])
        mv2 = sb("mv2", [P, T, 2])
        rs2 = sb("rs2", [P, 2, T])
        xn = sb("xn", [P, T, P])
        ht = sb("ht", [P, T * P])
        qk_neg = sb("qk_neg", [P, 2, T * P])
        qk_f = sb("qk_f", [P, 2, T * P])
        qk_hi = sb("qk_hi", [P, 2, T * P], F16)
        qk_lo = sb("qk_lo", [P, 2, T * P], F16)
        qkst = sb("qkst", [P, 2, G, T * P], F16)
        v_hl = sb("v_hl", [P, T, H, VC], F16)
        negm = sb("negm", [P, 2, 2, 2], F16)
        pf = sb("pf", [P, 2, 2, 3, P])
        p_hi = sb("p_hi", [P, 2, 2, 3, P], F16)
        p_lo = sb("p_lo", [P, 2, 2, 3, P], F16)
        pv_sb = sb("pv_sb", [P, T, H, VC])
        rden = sb("rden", [P, T, H])
        num = sb("num", [P, T, H, HD])
        cx = sb("cx", [P, T, P])
        cxt = sb("cxt", [P, T * P])
        n2 = sb("n2", [P, T, P])
        h2t = sb("h2t", [P, T * P])
        act_s = sb("act_s", [P, 2, CH * P])
        hid = sb("hid", [P, 2, CH * P])

        banks_n = ctx.enter_context(nc.psum_tensor("banks_n", [P, 2, 512], F32))
        banks_t = [ctx.enter_context(nc.psum_tensor(f"banks_t{i}", [P, 2, 512], F32)) for i in range(2)]
        bank_pv = ctx.enter_context(nc.psum_tensor("bank_pv", [P, 512], F32))
        mx = ctx.enter_context(nc.psum_tensor("bank_mx", [P, 512], F32))
        psum = [pair[:, n, :] for pair in (banks_n, *banks_t) for n in range(2)] + [bank_pv, mx]
        BANK_N, BANK_T, BANK_PV, BANK_MX = 0, 2, 6, 7

        def sem(name):
            return ctx.enter_context(nc.semaphore(name))

        x_in, w_in, consts, outs, passed = sem("x_in"), sem("w_in"), sem("consts"), sem("outs"), sem("passed")
        weights_in = 16 * 22

        def sems(n, names):
            return {name: sem(f"{name}_{n}") for name in names.split()}

        phases = [dict(soft=soft, w=0 if soft else 1, back_links=4 if soft else 2,
                                  norm_links=6 if soft else 1, **sems(
            n, "filled emptied stats rstd y_in y_bias xn_in hi_in neg_in exp_in full_in v_hi scored negm_in turned "
            "exped masked p_hi_in p_lo_in pv_done pv_out cx_in stats2 rstd2 n2_in cv_front cv_back cp_front cp_back "
            "h2_in")) for n, soft in enumerate((True, False, True))]
        mixtures = [dict(**sems(f"m{n}", "up_done silu_in hid_in down_done added route_in chain e_in done"))
                    for n in range(2)]
        block = ctx.enter_context(nc.Block())

        def apart(eng):
            eng.sem_inc(passed, 1)

        order = [("f7c", 0), ("f7d", 0), ("f5", 0), ("f1", 1), ("f3", 1), ("b1", -1), ("f7a", 1), ("b3", -1),
                 ("f7b", 1), ("b6", -1), ("b8", -1)]

        def fill_no(ph, b, name):
            def listed(first, last):
                return [n for n, of in order if not (first and of < 0) and not (last and of > 0)
                        and (ph["soft"] or n not in ("b6", "b8"))]
            pro = ["f1", "f3", "f7a", "f7b"]
            if isinstance(b, int) and b == -1:
                return pro.index(name)
            if isinstance(b, int) and b == 0:
                return 4 + listed(True, False).index(name)
            per = len(listed(False, False))
            base = 4 + len(listed(True, False)) - per
            if isinstance(b, int) and b == B:
                tail = [n for n in ("b1", "b3", "b6", "b8") if ph["soft"] or n in ("b1", "b3")]
                return base + per * (B - 1) + len(listed(False, True)) + tail.index(name)
            if isinstance(b, int) and b == B - 1:
                return base + per * b + listed(False, True).index(name)
            return b * per + (base + listed(False, False).index(name))


        @block.tensor
        def _(pe):
            def fill(ph, b, name):
                n = fill_no(ph, b, name)
                if not (isinstance(n, int) and n == 0):
                    pe.wait_ge(ph["emptied"], n)

            def front_turn(ph, b, it):
                pe.wait_ge(ph["xn_in"], b + 1)
                fill(ph, it, "f1")
                for t in range(T):
                    ins = nc.tensor.transpose(mx[:, t * P:(t + 1) * P], xn[:, t, :], ident[:, :])
                ins.then_inc(ph["filled"], 1)

            def front_qk(ph, b, it):
                fill(ph, it, "f3")
                for k in range(2):
                    ins = nc.tensor.matmul(mx[:, k * 256:(k + 1) * 256], w_qk[ph["w"]][:, k, :], ht[:, :],
                                           start=(k == 0), stop=True, skip_group_check=True)
                ins.then_inc(ph["filled"], 1)

            def front_spread(ph, b, it, name, k, gs):
                fill(ph, it, name)
                for n, g in enumerate(gs):
                    for part, src in enumerate((qk_hi, qk_lo)):
                        ins = nc.tensor.matmul(mx[:, n * 256:(n + 1) * 256],
                                               sel[:, k, part, g, :, :, :].rearrange("p a b c -> p (a b c)"),
                                               src[:, k, :], start=(n == 0 and part == 0), stop=(part == 1),
                                               skip_group_check=True)
                ins.then_inc(ph["filled"], 1)

            def front_v(ph, b):
                fill(ph, b, "f5")
                for t in range(T):
                    ins = nc.tensor.matmul(mx[:, t * P:(t + 1) * P], ht[:, t * P:(t + 1) * P], w_v[ph["w"]][:, :],
                                           start=(t == 0), stop=True, skip_group_check=True)
                ins.then_inc(ph["filled"], 1)

            def back_turn(ph, b, it):
                pe.wait_ge(ph["cx_in"], b + 1)
                fill(ph, it, "b1")
                for t in range(T):
                    ins = nc.tensor.transpose(mx[:, t * P:(t + 1) * P], cx[:, t, :], ident[:, :])
                ins.then_inc(ph["filled"], 1)

            def back_wo(ph, b, it):
                fill(ph, it, "b3")
                for t in range(T):
                    ins = nc.tensor.matmul(mx[:, t * P:(t + 1) * P], cxt[:, t * P:(t + 1) * P], w_o[ph["w"]][:, :],
                                           start=(t == 0), stop=True, skip_group_check=True)
                ins.then_inc(ph["filled"], 1)

            def back_h2(ph, b, it):
                pe.wait_ge(ph["n2_in"], b + 1)
                fill(ph, it, "b6")
                for t in range(T):
                    ins = nc.tensor.transpose(mx[:, t * P:(t + 1) * P], n2[:, t, :], ident[:, :])
                ins.then_inc(ph["filled"], 1)

            def back_gate(ph, b, it):
                fill(ph, it, "b8")
                for t in range(T):
                    ins = nc.tensor.matmul(mx[:, t * E:(t + 1) * E], h2t[:, t * P:(t + 1) * P], gw[:, :],
                                           start=(t == 0), stop=True, skip_group_check=True)
                ins.then_inc(ph["filled"], 1)

            def heads(s):
                return [(s // 2, 2 * (s % 2) + n) for n in range(2)]

            def part(k, g, j, t):
                return qkst[32 * j:32 * j + 24, k, g, t * P:(t + 1) * P]

            def natural(ph, b, s):
                if not (isinstance(b, int) and b == 0 and s == 0):
                    pe.wait_ge(ph["negm_in"], b * S + s)
                for n in range(2):
                    nc.tensor.matmul(psum[BANK_N + n][:, 0:2 * P], identb[:, :],
                                     maskb[:, :, :].rearrange("p a b -> p (a b)"),
                                     start=True, stop=False, skip_group_check=True)
                for n, (g, j) in enumerate(heads(s)):
                    for c, (tq, tk) in enumerate(((0, 0), (1, 1), (1, 0))):
                        ins = nc.tensor.matmul(psum[BANK_N + n][:, c * P:(c + 1) * P], part(0, g, j, tq),
                                               part(1, g, j, tk), start=False, stop=True, skip_group_check=True)
                ins.then_inc(ph["scored"], 1)

            def turned(ph, b, s):
                if ph["soft"]:
                    pe.wait_ge(ph["negm_in"], b * S + s + 1)
                if not (isinstance(b, int) and b == 0 and s < 2):
                    pe.wait_ge(ph["exped"], b * S + s - 1)
                for n, (g, j) in enumerate(heads(s)):
                    bank = psum[BANK_T + 2 * (s % 2) + n]
                    for c, (tk, tq) in enumerate(((0, 0), (1, 1), (0, 1))):
                        ins = nc.tensor.matmul(bank[:, c * P:(c + 1) * P], part(1, g, j, tk), part(0, g, j, tq),
                                               start=(c == 0), stop=not ph["soft"], skip_group_check=True)
                if ph["soft"]:
                    for n in range(2):
                        bank = psum[BANK_T + 2 * (s % 2) + n]
                        for c, tq in enumerate((0, 1, 1)):
                            ins = nc.tensor.matmul(bank[:, c * P:(c + 1) * P],
                                                   negm[:, s % 2, tq, n:n + 1].to_broadcast([P, P]), ident16[:, :],
                                                   start=False, stop=True, skip_group_check=True)
                ins.then_inc(ph["turned"], 1)

            def values(ph, b, s):
                pe.wait_ge(ph["p_lo_in"], b * S + s + 1)
                if s % 4 == 0 and not (isinstance(b, int) and b == 0 and s == 0):
                    pe.wait_ge(ph["pv_out"], 2 * b + s // 4)
                for n in range(2):
                    h = 2 * s + n
                    for tq, blocks in enumerate((((0, 0),), ((0, 2), (1, 1)))):
                        o = (tq * (H // 2) + h % (H // 2)) * VC
                        todo = [(src, tk, c) for tk, c in blocks for src in (p_hi, p_lo)]
                        for i, (src, tk, c) in enumerate(todo):
                            ins = nc.tensor.matmul(psum[BANK_PV][:, o:o + VC], src[:, s % 2, n, c, :],
                                                   v_hl[:, tk, h, :], start=(i == 0), stop=(i == len(todo) - 1),
                                                   skip_group_check=True)
                ins.then_inc(ph["pv_done"], 1)

            def iteration(ph, b, first=False, last=False):
                for s in range(S):
                    if ph["soft"] and s + 1 < S:
                        natural(ph, b, s + 1)
                    elif ph["soft"] and not last:
                        pe.wait_ge(ph["emptied"], fill_no(ph, b, "f7b") + 1)
                        natural(ph, b + 1, 0)
                    turned(ph, b, s)
                    if s < 2 and not first:
                        values(ph, b - 1, S - 2 + s)
                    if s == 2:
                        pe.wait_ge(ph["emptied"], fill_no(ph, b, "f5") + 1)
                    if s >= 2:
                        values(ph, b, s - 2)
                    if s == 0:
                        front_spread(ph, b, b, "f7c", 0, (2, 3))
                        front_spread(ph, b, b, "f7d", 1, (2, 3))
                    if s == 1:
                        front_v(ph, b)
                    if s == 2:
                        if not last:
                            front_turn(ph, b + 1, b)
                    if s == 3:
                        if not last:
                            front_qk(ph, b + 1, b)
                        if not first:
                            back_turn(ph, b - 1, b)
                        if last or first:
                            pe.wait_ge(ph["emptied"], fill_no(ph, b, "f7d") + 1)
                    if s == 4:
                        if not last:
                            front_spread(ph, b + 1, b, "f7a", 0, (0, 1))
                        if not first:
                            back_wo(ph, b - 1, b)
                    if s == 5 and not last:
                        front_spread(ph, b + 1, b, "f7b", 1, (0, 1))
                    if ph["soft"] and s == 6 and not first:
                        back_h2(ph, b - 1, b)
                    if ph["soft"] and s == 7 and not first:
                        back_gate(ph, b - 1, b)

            def attention(ph):
                front_turn(ph, 0, -1)
                front_qk(ph, 0, -1)
                front_spread(ph, 0, -1, "f7a", 0, (0, 1))
                front_spread(ph, 0, -1, "f7b", 1, (0, 1))
                pe.wait_ge(ph["emptied"], 4)
                if ph["soft"]:
                    natural(ph, 0, 0)
                iteration(ph, 0, first=True)
                with pe.Fori(1, B - 1) as b:
                    iteration(ph, b)
                iteration(ph, B - 1, last=True)
                for s in (S - 2, S - 1):
                    values(ph, B - 1, s)
                back_turn(ph, B - 1, B)
                back_wo(ph, B - 1, B)
                if ph["soft"]:
                    back_h2(ph, B - 1, B)
                    back_gate(ph, B - 1, B)

            def experts(m):
                K = E * HC

                def down(c, k):
                    e, hc = divmod(k, HC)
                    pe.wait_ge(m["hid_in"], c * K + k + 1)
                    if hc == 0 and not (isinstance(c, int) and c == 0 and e < 2):
                        pe.wait_ge(m["added"], c * E + e - 1)
                    for t in range(CH):
                        ins = nc.tensor.matmul(psum[4 + e % 2][:, t * P:(t + 1) * P],
                                               hid[:, k % 2, t * P:(t + 1) * P], w3s[:, e, hc, :],
                                               start=(hc == 0 and t == 0), stop=(hc == HC - 1), skip_group_check=True)
                    ins.then_inc(m["down_done"], 1)

                def chunk(c, first=False):
                    for k in range(K):
                        e, hc = divmod(k, HC)
                        if not (first and k < 2):
                            pe.wait_ge(m["hid_in"], c * K + k - 1)
                        for w in range(2):
                            ins = nc.tensor.matmul(psum[2 * (k % 2) + w][:, :], w12[:, e, w, hc * P:(hc + 1) * P],
                                                   h2t_all[:, bass.ds(c * CH, CH), :].rearrange("p a b -> p (a b)"),
                                                   start=True, stop=True)
                        ins.then_inc(m["up_done"], 1)
                        if k:
                            down(c, k - 1)
                        elif not first:
                            down(c - 1, K - 1)
                chunk(0, first=True)
                with pe.Fori(1, NT // CH) as c:
                    chunk(c)
                down(NT // CH - 1, K - 1)

            pe.wait_ge(w_in, weights_in)
            pe.wait_ge(consts, 1)
            for n, ph in enumerate(phases):
                attention(ph)
                if ph["soft"]:
                    pe.wait_ge(ph["h2_in"], B)
                    experts(mixtures[n // 2])

        @block.scalar
        def _(sc):
            def empty(ph, it, name, ins_f):
                sc.wait_ge(ph["filled"], fill_no(ph, it, name) + 1)
                ins_f().then_inc(ph["emptied"], 1)

            def spread(ph, it, name, k, g):
                empty(ph, it, name, lambda: nc.scalar.copy(
                    qkst[:, k, g:g + 2, :].rearrange("p a b -> p (a b)"), mx[:, :]))

            def qk_high(ph, b, it):
                if ph["soft"]:
                    sc.wait_ge(ph["filled"], fill_no(ph, it, "f3") + 1)
                    nc.scalar.copy(qk_hi[:, :, :].rearrange("p a b -> p (a b)"), mx[:, :]).then_inc(ph["hi_in"], 1)
                else:
                    sc.wait_ge(ph["neg_in"], b + 1)
                    nc.scalar.activation(qk_neg[:, :, :], qk_neg[:, :, :], ACT.Exp).then_inc(ph["exp_in"], 1)
                    sc.wait_ge(ph["full_in"], b + 1)
                    nc.scalar.copy(qk_hi[:, :, :], qk_f[:, :, :]).then_inc(ph["hi_in"], 1)

            def v_high(ph, b):
                sc.wait_ge(ph["filled"], fill_no(ph, b, "f5") + 1)
                nc.scalar.copy(v_hl[:, :, :, 0:HD], mx[:, 0:T * P].rearrange("p (t h d) -> p t h d", t=T, h=H))\
                    .then_inc(ph["v_hi"], 1)

            def exps(ph, b, s):
                sc.wait_ge(ph["turned"], b * S + s + 1)
                if not (isinstance(b, int) and b == 0 and s < 2):
                    sc.wait_ge(ph["p_lo_in"], b * S + s - 1)
                src = banks_t[s % 2][:, :, 0:3 * P]
                nc.scalar.activation(pf[:, s % 2, :, :, :].rearrange("p a b c -> p a (b c)"), src,
                                     ACT.Exp if ph["soft"] else ACT.Copy,
                                     scale=HD ** -0.5 if ph["soft"] else 1.0).then_inc(ph["exped"], 1)

            def p_high(ph, b, s):
                sc.wait_ge(ph["masked"], b * S + s + 1)
                if not (isinstance(b, int) and b == 0 and s < 2):
                    sc.wait_ge(ph["pv_done"], b * S + s - 1)
                nc.scalar.copy(p_hi[:, s % 2, :, :, :], pf[:, s % 2, :, :, :]).then_inc(ph["p_hi_in"], 1)

            def pv_read(ph, b, hf):
                sc.wait_ge(ph["pv_done"], b * S + 4 * (hf + 1))
                nc.scalar.copy(pv_sb[:, :, hf * 8:(hf + 1) * 8, :],
                               psum[BANK_PV][:, 0:T * 8 * VC].rearrange("p (t h d) -> p t h d", t=T, h=8))\
                    .then_inc(ph["pv_out"], 1)

            def ctx_turned(ph, b, it):
                empty(ph, it, "b1", lambda: nc.scalar.copy(cxt[:, :], mx[:, 0:T * P]))

            def h2_turned(ph, b, it):
                sc.wait_ge(ph["filled"], fill_no(ph, it, "b6") + 1)
                nc.scalar.activation(h2t_all[:, bass.ds(2 * b, 2), :].rearrange("p a b -> p (a b)"), mx[:, 0:T * P],
                                     ACT.Identity, scale=ln[:, 2:3], bias=ln[:, 3:4]).then_inc(ph["h2_in"], 1)
                nc.scalar.activation(h2t[:, :], mx[:, 0:T * P], ACT.Identity,
                                     scale=ln[:, 2:3], bias=ln[:, 3:4]).then_inc(ph["emptied"], 1)

            def iteration(ph, b, first=False, last=False):
                for s in range(S):
                    if s:
                        p_high(ph, b, s - 1)
                    elif not first:
                        p_high(ph, b - 1, S - 1)
                    exps(ph, b, s)
                    if s == 0:
                        spread(ph, b, "f7c", 0, 2)
                    if s == 1:
                        v_high(ph, b)
                        if not first:
                            pv_read(ph, b - 1, 1)
                    if s == 3:
                        if not last:
                            qk_high(ph, b + 1, b)
                        if not first:
                            ctx_turned(ph, b - 1, b)
                    if s == 4 and not last:
                        spread(ph, b, "f7a", 0, 0)
                    if s == 5:
                        if not last:
                            spread(ph, b, "f7b", 1, 0)
                        pv_read(ph, b, 0)
                    if ph["soft"] and s == 6 and not first:
                        h2_turned(ph, b - 1, b)

            def attention(ph):
                qk_high(ph, 0, -1)
                spread(ph, -1, "f7a", 0, 0)
                spread(ph, -1, "f7b", 1, 0)
                iteration(ph, 0, first=True)
                with sc.Fori(1, B - 1) as b:
                    iteration(ph, b)
                iteration(ph, B - 1, last=True)
                p_high(ph, B - 1, S - 1)
                pv_read(ph, B - 1, 1)
                ctx_turned(ph, B - 1, B)
                if ph["soft"]:
                    h2_turned(ph, B - 1, B)

            def experts(m):
                K = E * HC
                sc.wait_ge(m["route_in"], 1)
                nc.scalar.activation(prob[:, :, 0], prob[:, :, 0], ACT.Exp).then_inc(m["e_in"], 1)

                def chunk(c, first=False):
                    for k in range(K):
                        sc.wait_ge(m["up_done"], c * K + k + 1)
                        if not (first and k < 2):
                            sc.wait_ge(m["hid_in"], c * K + k - 1)
                        nc.scalar.activation(act_s[:, k % 2, :], psum[2 * (k % 2)][:, :], ACT.Silu)\
                            .then_inc(m["silu_in"], 1)
                chunk(0, first=True)
                with sc.Fori(1, NT // CH) as c:
                    chunk(c)

            sc.wait_ge(w_in, weights_in)
            for n, ph in enumerate(phases):
                attention(ph)
                if ph["soft"]:
                    experts(mixtures[n // 2])

        @block.vector
        def _(ve):
            def front_stats(ph, b):
                c = Chain(ve, ph["cv_front"], b * FRONT_V)
                apart(ve)
                for t in range(T):
                    ins = nc.vector.bn_stats(st[:, t, :], x_all[:, b, t, :])
                    if t == 0:
                        c.link(ins)
                        apart(ve)
                c.link(ins)
                apart(ve)
                nc.vector.bn_aggr(mv[:, 0, :], st[:, 0, :])
                nc.vector.bn_aggr(mv[:, 1, :], st[:, 1, :]).then_inc(ph["stats"], 1)

            def front_norm(ph, b):
                c = Chain(ve, ph["cv_front"], b * FRONT_V)
                c.n = 2
                ve.wait_ge(ph["rstd"], b + 1)
                if ph["soft"]:
                    for t in range(T):
                        ins = nc.vector.tensor_scalar(y_all[:, b, t, :], x_all[:, b, t, :], mv[:, t, 0:1],
                                                      rs[:, 1, t:t + 1], ALU.subtract, ALU.mult)
                    ins.then_inc(ph["y_in"], 1)
                for t in range(T):
                    ins = nc.vector.tensor_scalar(xn[:, t, :], x_all[:, b, t, :], mv[:, t, 0:1],
                                                  rs[:, 5 if ph["soft"] else 1, t:t + 1], ALU.subtract, ALU.mult)
                ins.then_inc(ph["xn_in"], 1)

            def front_ht(ph, b, it):
                ve.wait_ge(ph["filled"], fill_no(ph, it, "f1") + 1)
                if ph["soft"]:
                    nc.vector.tensor_scalar(ht[:, :], mx[:, 0:T * P], ln[:, 0:1], ln[:, 1:2], ALU.mult, ALU.add)\
                        .then_inc(ph["emptied"], 1)
                else:
                    nc.vector.tensor_copy(ht[:, :], mx[:, 0:T * P]).then_inc(ph["emptied"], 1)

            def qk_low(ph, b, it):
                flat = "p a b -> p (a b)"
                if ph["soft"]:
                    ve.wait_ge(ph["hi_in"], b + 1)
                    nc.vector.tensor_tensor(qk_lo[:, :, :].rearrange(flat), mx[:, :], qk_hi[:, :, :].rearrange(flat),
                                            ALU.subtract).then_inc(ph["emptied"], 1)
                    return
                ve.wait_ge(ph["filled"], fill_no(ph, it, "f3") + 1)
                nc.vector.tensor_scalar(qk_neg[:, :, :].rearrange(flat), mx[:, :], 0.0, None, ALU.min)\
                    .then_inc(ph["neg_in"], 1)
                ve.wait_ge(ph["exp_in"], b + 1)
                nc.vector.scalar_tensor_tensor(qk_f[:, :, :].rearrange(flat), mx[:, :], 0.0,
                                               qk_neg[:, :, :].rearrange(flat), ALU.max, ALU.add)\
                    .then_inc(ph["full_in"], 1)
                ve.wait_ge(ph["hi_in"], b + 1)
                nc.vector.tensor_tensor(qk_lo[:, :, :].rearrange(flat), qk_f[:, :, :].rearrange(flat),
                                        qk_hi[:, :, :].rearrange(flat), ALU.subtract).then_inc(ph["emptied"], 1)

            def spread(ph, it, name, k, g):
                ve.wait_ge(ph["filled"], fill_no(ph, it, name) + 1)
                nc.vector.tensor_copy(qkst[:, k, g:g + 2, :].rearrange("p a b -> p (a b)"), mx[:, :])\
                    .then_inc(ph["emptied"], 1)

            def v_low(ph, b):
                ve.wait_ge(ph["v_hi"], b + 1)
                nc.vector.tensor_tensor(v_hl[:, :, :, HD + 1:VC],
                                        mx[:, 0:T * P].rearrange("p (t h d) -> p t h d", t=T, h=H),
                                        v_hl[:, :, :, 0:HD], ALU.subtract).then_inc(ph["emptied"], 1)

            def maxima(ph, b, s):
                ve.wait_ge(ph["scored"], b * S + s + 1)
                nc.vector.tensor_reduce(negm[:, s % 2, 0, :], banks_n[:, :, 0:P], AX.X, ALU.max, negate=True)
                nc.vector.tensor_reduce(negm[:, s % 2, 1, :], banks_n[:, :, P:3 * P], AX.X, ALU.max, negate=True)\
                    .then_inc(ph["negm_in"], 1)

            def p_low(ph, b, s):
                ve.wait_ge(ph["p_hi_in"], b * S + s + 1)
                flat = "p a b c -> p (a b c)"
                nc.vector.tensor_tensor(p_lo[:, s % 2, :, :, :].rearrange(flat), pf[:, s % 2, :, :, :].rearrange(flat),
                                        p_hi[:, s % 2, :, :, :].rearrange(flat), ALU.subtract).then_inc(ph["p_lo_in"], 1)

            def back_context(ph, b):
                c = Chain(ve, ph["cv_back"], b * ph["back_links"])
                ve.wait_ge(ph["pv_out"], 2 * b + 2)
                if ph["soft"]:
                    c.link(nc.vector.tensor_tensor(num[:, :, :, :], pv_sb[:, :, :, 0:HD], pv_sb[:, :, :, HD + 1:VC],
                                                   ALU.add))
                    c.link(nc.vector.reciprocal(rden[:, :, :], pv_sb[:, :, :, HD]))
                else:
                    c.link(nc.vector.tensor_scalar(rden[:, :, :], pv_sb[:, :, :, HD], 1e-6, None, ALU.max))
                    nc.vector.tensor_tensor(num[:, :, :, :], pv_sb[:, :, :, 0:HD], pv_sb[:, :, :, HD + 1:VC], ALU.add)
                    c.link(nc.vector.reciprocal(rden[:, :, :], rden[:, :, :]))
                nc.vector.tensor_tensor(cx[:, :, :].rearrange("p t (h d) -> p t h d", h=H), num[:, :, :, :],
                                        rden[:, :, :].unsqueeze(3).to_broadcast([P, T, H, HD]), ALU.mult)\
                    .then_inc(ph["cx_in"], 1)

            def back_add(ph, b, it):
                ve.wait_ge(ph["filled"], fill_no(ph, it, "b3") + 1)
                src = mx[:, 0:T * P].rearrange("p (t d) -> p t d", t=T)
                if not ph["soft"]:
                    nc.vector.tensor_tensor(x_all[:, b, :, :], src, x_all[:, b, :, :], ALU.add)\
                        .then_inc(ph["emptied"], 1)
                    return
                c = Chain(ve, ph["cv_back"], b * ph["back_links"])
                c.n = 2
                ve.wait_ge(ph["y_bias"], b + 1)
                nc.vector.tensor_tensor(y_all[:, b, :, :], src, y_all[:, b, :, :], ALU.add).then_inc(ph["emptied"], 1)
                ve.wait_ge(ph["emptied"], fill_no(ph, it, "b3") + 1)
                for t in range(T):
                    apart(ve)
                    c.link(nc.vector.bn_stats(st2[:, t, :], y_all[:, b, t, :]))
                apart(ve)
                nc.vector.bn_aggr(mv2[:, 0, :], st2[:, 0, :])
                nc.vector.bn_aggr(mv2[:, 1, :], st2[:, 1, :]).then_inc(ph["stats2"], 1)
                c.end(ph["back_links"])

            def back_norm(ph, b):
                ve.wait_ge(ph["rstd2"], b + 1)
                for t in range(T):
                    ins = nc.vector.tensor_scalar(n2[:, t, :], y_all[:, b, t, :], mv2[:, t, 0:1],
                                                  rs2[:, 1, t:t + 1], ALU.subtract, ALU.mult)
                ins.then_inc(ph["n2_in"], 1)

            def back_gate(ph, b, it):
                ve.wait_ge(ph["filled"], fill_no(ph, it, "b8") + 1)
                nc.vector.tensor_copy(gates[:, bass.ds(2 * b, 2), :].rearrange("p a b -> p (a b)"), mx[:, 0:T * E])\
                    .then_inc(ph["emptied"], 1)

            def iteration(ph, b, first=False, last=False):
                for s in range(S):
                    if ph["soft"] and s + 1 < S:
                        maxima(ph, b, s + 1)
                    elif ph["soft"] and not last:
                        maxima(ph, b + 1, 0)
                    if s:
                        p_low(ph, b, s - 1)
                    elif not first:
                        p_low(ph, b - 1, S - 1)
                    if s == 0:
                        spread(ph, b, "f7d", 1, 2)
                        if not last:
                            front_stats(ph, b + 1)
                    if s == 1:
                        v_low(ph, b)
                        if not last:
                            front_norm(ph, b + 1)
                    if s == 2:
                        if not last:
                            front_ht(ph, b + 1, b)
                        if not first:
                            back_context(ph, b - 1)
                    if s == 3 and not last:
                        qk_low(ph, b + 1, b)
                    if s == 4 and not first:
                        back_add(ph, b - 1, b)
                    if ph["soft"] and s == 5 and not first:
                        back_norm(ph, b - 1)
                    if ph["soft"] and s == 7 and not first:
                        back_gate(ph, b - 1, b)

            def attention(ph):
                front_stats(ph, 0)
                front_norm(ph, 0)
                front_ht(ph, 0, -1)
                qk_low(ph, 0, -1)
                if ph["soft"]:
                    maxima(ph, 0, 0)
                iteration(ph, 0, first=True)
                with ve.Fori(1, B - 1) as b:
                    iteration(ph, b)
                iteration(ph, B - 1, last=True)
                p_low(ph, B - 1, S - 1)
                back_context(ph, B - 1)
                back_add(ph, B - 1, B)
                if ph["soft"]:
                    back_norm(ph, B - 1)
                    back_gate(ph, B - 1, B)

            def experts(ph, m):
                c = Chain(ve, m["chain"], 0)
                ve.wait_ge(ph["emptied"], fill_no(ph, B, "b8") + 1)
                for n in range(NT):
                    ins = nc.vector.max(top[:, n, :], gates[:, n, :])
                c.link(ins)
                for n in range(NT):
                    ins = nc.vector.max_index(topi[:, n, :], top[:, n, :], gates[:, n, :])
                nc.vector.tensor_tensor(prob[:, :, 0], top[:, :, 1], top[:, :, 0], ALU.subtract)\
                    .then_inc(m["route_in"], 1)
                c.link(ins)
                c.link(nc.vector.tensor_copy(topf[:, :, :], topi[:, :, 0:2]))
                ve.wait_ge(m["e_in"], 1)
                c.link(nc.vector.tensor_scalar(prob[:, :, 1], prob[:, :, 0], 1.0, None, ALU.add))
                c.link(nc.vector.reciprocal(prob[:, :, 1], prob[:, :, 1]))
                c.link(nc.vector.tensor_tensor(prob[:, :, 2], prob[:, :, 0], prob[:, :, 1], ALU.mult))
                for k, dst in ((0, route), (1, onehot)):
                    c.link(nc.vector.tensor_tensor(dst[:, :, :], iota_e[:, :].unsqueeze(1).to_broadcast([P, NT, E]),
                                                   topf[:, :, k:k + 1].to_broadcast([P, NT, E]), ALU.is_equal))
                    c.link(nc.vector.tensor_tensor(dst[:, :, :], dst[:, :, :],
                                                   prob[:, :, k + 1:k + 2].to_broadcast([P, NT, E]), ALU.mult))
                c.link(nc.vector.tensor_tensor(route[:, :, :], route[:, :, :], onehot[:, :, :], ALU.add))
                K = E * HC

                def product(cc, k):
                    ve.wait_ge(m["silu_in"], cc * K + k + 1)
                    if not (isinstance(cc, int) and cc == 0 and k < 2):
                        ve.wait_ge(m["down_done"], cc * K + k - 1)
                    nc.vector.tensor_tensor(hid[:, k % 2, :], psum[2 * (k % 2) + 1][:, :], act_s[:, k % 2, :],
                                            ALU.mult).then_inc(m["hid_in"], 1)

                def add(cc, e):
                    ve.wait_ge(m["down_done"], cc * K + HC * (e + 1))
                    if not (isinstance(cc, int) and cc == 0 and e == 0):
                        ve.wait_ge(m["added"], cc * E + e)
                    for t in range(CH):
                        y = y_all[:, :, :, :].rearrange("p b t d -> p (b t) d")[:, bass.ds(cc * CH + t, 1), :]\
                            .rearrange("p a d -> p (a d)")
                        r = route[:, bass.ds(cc * CH + t, 1), e:e + 1].rearrange("p a b -> p (a b)")
                        ins = nc.vector.scalar_tensor_tensor(y, psum[4 + e % 2][:, t * P:(t + 1) * P], r, y,
                                                             ALU.mult, ALU.add)
                    ins.then_inc(m["added"], 1)

                def chunk(cc, first=False):
                    for k in range(K):
                        product(cc, k)
                        if k >= 2 and k % 2 == 0:
                            add(cc, k // 2 - 1)
                        if k == 0 and not first:
                            add(cc - 1, E - 1)
                chunk(0, first=True)
                with ve.Fori(1, NT // CH) as cc:
                    chunk(cc)
                add(NT // CH - 1, E - 1)
                ve.wait_ge(m["added"], NT // CH * E)
                flat = "p b t d -> p (b t d)"
                nc.vector.scalar_tensor_tensor(x_all[:, :, :, :].rearrange(flat), y_all[:, :, :, :].rearrange(flat),
                                               0.5, x_all[:, :, :, :].rearrange(flat), ALU.mult, ALU.add)\
                    .then_inc(m["done"], 1)
                ve.wait_ge(m["done"], 1)

            ve.wait_ge(x_in, 16)
            ve.wait_ge(w_in, weights_in)
            ve.wait_ge(consts, 1)
            for n, ph in enumerate(phases):
                attention(ph)
                if not ph["soft"]:
                    ve.wait_ge(ph["emptied"], fill_no(ph, B, "b3") + 1)
                if ph["soft"]:
                    experts(ph, mixtures[n // 2])

        @block.gpsimd
        def _(gp):
            pools = sem("pools")
            c = Chain(gp, pools, 0)

            def diag(t, fill=1.0):
                c.link(nc.gpsimd.memset(t, 0.0))
                c.link(nc.gpsimd.affine_select(out=t, in_=t, pattern=[[-1, P]], compare_op=ALU.not_equal, fill=fill,
                                               base=0, channel_multiplier=1))
            diag(ident[:, :])
            diag(ident16[:, :])
            diag(identb[:, :])
            c.link(nc.gpsimd.memset(maskb[:, :, :], 0.0))
            c.link(nc.gpsimd.affine_select(out=maskb[:, :, :], in_=maskb[:, :, :], pattern=[[0, 2], [-1, P]],
                                           compare_op=ALU.is_ge, fill=BIG, base=0, channel_multiplier=1))
            c.link(nc.gpsimd.memset(sel[:, :, :, :, :, :, :], 0.0))
            for k, rows in enumerate((((0, 1), (2,)), ((0, 2), (1,)))):
                for part, blocks in enumerate(rows):
                    for r in blocks:
                        at = sel[:, k, part, :, :, r, :]
                        c.link(nc.gpsimd.affine_select(out=at, in_=at, pattern=[[-32, G], [-8, 4], [-1, HD]],
                                                       compare_op=ALU.not_equal, fill=1.0, base=0,
                                                       channel_multiplier=1))
            c.link(nc.gpsimd.memset(v_hl[:, :, :, :], 1.0))
            c.link(nc.gpsimd.memset(half[:, :], -0.5))
            nc.gpsimd.iota(iota_e[:, :], pattern=[[1, E]], base=0, channel_multiplier=0,
                           allow_small_or_imprecise_dtypes=True).then_inc(consts, 1)

            def front_rstd(ph, b):
                c = Chain(gp, ph["cp_front"], b * ph["norm_links"])
                gp.wait_ge(ph["stats"], b + 1)
                apart(gp)
                c.link(nc.gpsimd.tensor_scalar(rs[:, 0, :], mv[:, :, 1], EPS, None, ALU.add))
                if not ph["soft"]:
                    nc.gpsimd.tensor_tensor(rs[:, 1, :], rs[:, 0, :], half[:, :], ALU.pow).then_inc(ph["rstd"], 1)
                    return
                c.link(nc.gpsimd.tensor_tensor(rs[:, 1, :], rs[:, 0, :], half[:, :], ALU.pow))
                c.link(nc.gpsimd.tensor_tensor(rs[:, 2, :], mv[:, :, 1], rs[:, 1, :], ALU.mult))
                c.link(nc.gpsimd.tensor_tensor(rs[:, 2, :], rs[:, 2, :], rs[:, 1, :], ALU.mult))
                apart(gp)
                c.link(nc.gpsimd.tensor_scalar(rs[:, 3, :], rs[:, 2, :], EPS, None, ALU.add))
                c.link(nc.gpsimd.tensor_tensor(rs[:, 4, :], rs[:, 3, :], half[:, :], ALU.pow))
                nc.gpsimd.tensor_tensor(rs[:, 5, :], rs[:, 4, :], rs[:, 1, :], ALU.mult).then_inc(ph["rstd"], 1)

            def front_bias(ph, b):
                gp.wait_ge(ph["y_in"], b + 1)
                nc.gpsimd.tensor_tensor(y_all[:, b, :, :], y_all[:, b, :, :],
                                        bo_b[:, :].unsqueeze(1).to_broadcast([P, T, P]), ALU.add)\
                    .then_inc(ph["y_bias"], 1)

            def back_rstd(ph, b):
                c = Chain(gp, ph["cp_back"], b)
                gp.wait_ge(ph["stats2"], b + 1)
                apart(gp)
                c.link(nc.gpsimd.tensor_scalar(rs2[:, 0, :], mv2[:, :, 1], EPS, None, ALU.add))
                nc.gpsimd.tensor_tensor(rs2[:, 1, :], rs2[:, 0, :], half[:, :], ALU.pow).then_inc(ph["rstd2"], 1)

            def causal(ph, b, s):
                gp.wait_ge(ph["exped"], b * S + s + 1)
                apart(gp)
                at = pf[:, s % 2, :, 0:2, :].rearrange("p a b c -> p a (b c)")
                nc.gpsimd.affine_select(out=at, in_=at, pattern=[[0, 2], [0, 2], [1, P]], compare_op=ALU.is_ge,
                                        fill=0.0, base=0, channel_multiplier=-1).then_inc(ph["masked"], 1)

            def iteration(ph, b, first=False, last=False):
                for s in range(S):
                    causal(ph, b, s)
                    if s == 0 and not last:
                        front_rstd(ph, b + 1)
                    if ph["soft"] and s == 2 and not last:
                        front_bias(ph, b + 1)
                    if ph["soft"] and s == 4 and not first:
                        back_rstd(ph, b - 1)

            def attention(ph):
                front_rstd(ph, 0)
                if ph["soft"]:
                    front_bias(ph, 0)
                iteration(ph, 0, first=True)
                with gp.Fori(1, B - 1) as b:
                    iteration(ph, b)
                iteration(ph, B - 1, last=True)
                if ph["soft"]:
                    back_rstd(ph, B - 1)

            gp.wait_ge(w_in, weights_in)
            for ph in phases:
                attention(ph)

        @block.sync
        def _(sy):
            sy.dma_start(x_all[:, :, :, :], x.rearrange("b (t p) d -> p b t d", p=P)).then_inc(x_in, 16)
            n = 0
            for k, (q_, k_, v_, o_) in enumerate(((wq, wk, wv, wo), (Wq, Wk, Wv, Wo))):
                for dst, src in ((w_qk[k][:, 0, :], q_), (w_qk[k][:, 1, :], k_), (w_v[k][:, :], v_), (w_o[k][:, :], o_)):
                    sy.dma_start(dst, src).then_inc(w_in, 16)
                    n += 1
            for k, src in enumerate((ln1_s, ln1_b, ln2_s, ln2_b)):
                sy.dma_start(ln[:, k:k + 1], src.rearrange("(p a) -> p a", a=1)).then_inc(w_in, 16)
                n += 1
            sy.dma_start(bo_b[:, :], bo.unsqueeze(0).to_broadcast([P, P])).then_inc(w_in, 16)
            sy.dma_start(gw[:, :], gate_w).then_inc(w_in, 16)
            n += 2
            for e0 in (0, 4):
                for k, src in enumerate((w1, w2)):
                    sy.dma_start(w12[:, e0:e0 + 4, k, :], src[e0:e0 + 4].rearrange("e d h -> d e h"))\
                        .then_inc(w_in, 16)
                    n += 1
            for c in range(HC):
                for e0 in (0, 4):
                    sy.dma_start(w3s[:, e0:e0 + 4, c, :],
                                 w3[e0:e0 + 4, c * P:(c + 1) * P, :].rearrange("e h d -> h e d")).then_inc(w_in, 16)
                    n += 1
            assert n * 16 == weights_in, n
            sy.wait_ge(mixtures[1]["done"], 1)
            sy.dma_start(out.rearrange("b (t p) d -> p b t d", p=P), x_all[:, :, :, :]).then_inc(outs, 16)
            sy.wait_ge(outs, 16)


_INS = ["L0_attn_x", "L0_attn_Wq", "L0_attn_Wk", "L0_attn_Wv", "L0_attn_Wo", "L0_ffn_ln1_scale", "L0_ffn_ln1_shift",
        "L0_ffn_wq", "L0_ffn_wk", "L0_ffn_wv", "L0_ffn_wo", "L0_ffn_bo", "L0_ffn_ln2_scale", "L0_ffn_ln2_shift",
        "L0_ffn_gate_w", "L0_ffn_w1", "L0_ffn_w2", "L0_ffn_w3"]


def kernel(**inputs):
    import numpy as np
    import concourse.bacc as bacc
    from concourse.bass_utils import run_bass_kernel_spmd

    nc = bacc.Bacc("TRN2", target_bir_lowering=False, num_devices=1)
    arrays, args = {}, []
    for name in _INS:
        a = np.asarray(inputs[name])
        if name.startswith("L0_attn_W"):
            a = a.T
        arrays[name] = np.ascontiguousarray(a)
        args.append(nc.dram_tensor(name, a.shape, F32, kind="ExternalInput").ap())
    args.append(nc.dram_tensor("out", inputs["L0_attn_x"].shape, F32, kind="ExternalOutput").ap())
    build(nc, *args)
    return run_bass_kernel_spmd(nc, [arrays], core_ids=[0]).results[0]["out"]
```

```python
from contextlib import ExitStack

import concourse.bass as bass
from concourse import mybir

F32 = mybir.dt.float32
F16 = mybir.dt.float16
BF16 = mybir.dt.bfloat16
U32 = mybir.dt.uint32
ALU = mybir.AluOpType
ACT = mybir.ActivationFunctionType
AX = mybir.AxisListType

P = 128
B = 16
T = 2
NT = B * T
H = 16
HD = P // H
G = 4
S = G
GH = H // G
LOADS = 16 * 5
VC = 2 * HD + 1
E = 8
HID = 256
HC = HID // P
CH = 4
EPS = 1e-5
STATS = (range(0, 6), range(6, NT))
BIG = -1e30


class Chain:

    def __init__(self, eng, sem, base):
        self.eng, self.sem, self.base, self.n = eng, sem, base, 0

    def link(self, ins):
        ins.then_inc(self.sem, 1)
        self.n += 1
        self.eng.wait_ge(self.sem, self.base + self.n)

    def end(self, n):
        assert self.n == n, (self.n, n)


def tile_at(array, b):
    return array[:, b, :, :]


def build(nc, x, Wq, Wk, Wv, Wo, ln1_s, ln1_b, wq, wk, wv, wo, bo, ln2_s, ln2_b, gate_w, w1, w2, w3, out):
    ctx = ExitStack()

    def sb(name, shape, dt=F32):
        return ctx.enter_context(nc.sbuf_tensor(name, shape, dt))

    with ctx:
        x_all = sb("x_all", [P, B, T, P])
        yb = sb("yb", [P, T, P])
        y2 = sb("y2", [P, T, P])
        h2t_all = sb("h2t_all", [P, NT, P])
        gates = sb("gates", [P, NT, E])
        route = sb("route", [P, NT, E])
        top = sb("top", [P, NT, 8])
        topi = sb("topi", [P, NT, 8], U32)
        topf = sb("topf", [P, NT, 2])
        prob = sb("prob", [P, NT, 3])
        onehot = sb("onehot", [P, NT, E])
        w_qk = [sb(f"w_qk{n}", [P, 2, P]) for n in range(2)]
        w_v = [sb(f"w_v{n}", [P, P]) for n in range(2)]
        w_o = [sb(f"w_o{n}", [P, P]) for n in range(2)]
        ln = sb("ln", [P, 4])
        bo_b = sb("bo_b", [P, P])
        gw = sb("gw", [P, E])
        w12 = sb("w12", [P, E, 2, HID])
        w3s = sb("w3s", [P, E, HC, P])
        ident = sb("ident", [P, P])
        ident16 = sb("ident16", [P, P], F16)
        identb = sb("identb", [P, P], BF16)
        maskb = sb("maskb", [P, GH, P], BF16)
        sel = sb("sel", [P, 2, 2, G, 4, 4, HD], F16)
        iota_e = sb("iota_e", [P, E])
        half = sb("half", [P, NT])
        st = sb("st", [P, NT, 6])
        mv = sb("mv", [P, NT, 2])
        rs = sb("rs", [P, 6, NT])
        st2 = sb("st2", [P, T, 6])
        mv2 = sb("mv2", [P, T, 2])
        rs2 = sb("rs2", [P, 2, T])
        xn = sb("xn", [P, T, P])
        ht = sb("ht", [P, T * P])
        q_all = sb("q_all", [P, B, G, T * P], F16)
        k_all = sb("k_all", [P, B, G, T * P], F16)
        v_all = sb("v_all", [P, B, T, H, VC], F16)
        kst = sb("kst", [P, G, T * P], F16)
        qst = sb("qst", [P, G, GH, T * P], F16)
        v_hl = sb("v_hl", [P, T, H, VC], F16)
        negm = sb("negm", [P, 2, T, GH], F16)
        pf = sb("pf", [P, 2, 3, GH, P])
        p_hi = sb("p_hi", [P, 2, 3, GH, P], F16)
        p_lo = sb("p_lo", [P, 2, 3, GH, P], F16)
        pv_sb = sb("pv_sb", [P, T, H, VC])
        rden = sb("rden", [P, T, H])
        num = sb("num", [P, T, H, HD])
        cx = sb("cx", [P, T, P])
        cxt = sb("cxt", [P, T * P])
        n2 = sb("n2", [P, T, P])
        h2t = sb("h2t", [P, T * P])
        qk_hi, qk_lo = [a[:, :, :, :, :].rearrange("p a b c d -> p (a b c d)")[:, 0:2 * 2 * T * P]
                        .rearrange("p (n k m) -> p n k m", n=2, k=2) for a in (p_hi, p_lo)]
        qk_f = pf[:, :, :, :, :].rearrange("p a b c d -> p (a b c d)")[:, 0:2 * T * P]\
            .rearrange("p (k m) -> p k m", k=2)
        spare = pf[:, :, :, :, :].rearrange("p a b c d -> p (a b c d)")
        act_s = spare[:, 0:2 * CH * P].rearrange("p (a b) -> p a b", a=2)
        hid = spare[:, 2 * CH * P:4 * CH * P].rearrange("p (a b) -> p a b", a=2)

        banks_n = ctx.enter_context(nc.psum_tensor("banks_n", [P, 3, 512], F32))
        banks_t = ctx.enter_context(nc.psum_tensor("banks_t", [P, 3, 512], F32))
        bank_pv = ctx.enter_context(nc.psum_tensor("bank_pv", [P, 512], F32))
        mx = ctx.enter_context(nc.psum_tensor("bank_mx", [P, 512], F32))
        psum = [banks_n[:, n, :] for n in range(3)] + [banks_t[:, n, :] for n in range(3)]

        def sem(name):
            return ctx.enter_context(nc.semaphore(name))

        x_in, w_in, consts, outs, passed = [sem("tokens_in_0"), sem("tokens_in_1")], sem("w_in"), sem("consts"), sem("outs"), sem("passed")
        w_moe = sem("w_moe")
        weights_in, moe_in = 16 * 14, 16 * 8

        def sems(n, names):
            return {name: sem(f"{name}_{n}") for name in names.split()}

        both = ("filled emptied stats rstd xn_in hi_in v_hi turned exped p_hi_in p_lo_in pv_done pv_out cx_in cv_back "
                "cp_front ht_in v_done qk_done v_out qk_out spread_done act_spread dve_spread turn_done ")
        of_soft = both + "y_in y_bias scored negm_in masked stats2 rstd2 n2_in cp_back x_in h2_in"
        of_linear = both + "neg_in exp_in full_in"
        phases = [dict(soft=soft, w=0 if soft else 1, back_links=4 if soft else 2,
                       **sems(n, of_soft if soft else of_linear)) for n, soft in enumerate((True, False, True))]
        mixtures = [dict(**sems(f"m{n}", "up_done silu_in hid_in down_done added route_in chain e_in"))
                    for n in range(2)]
        for n, ph in enumerate(phases):
            ph["qk_loaded"] = [sem(f"qk_loaded_{n}_{hf}") for hf in range(2)]
            ph["v_loaded"] = [sem(f"v_loaded_{n}_{hf}") for hf in range(2)]
        block = ctx.enter_context(nc.Block())

        def apart(eng):
            eng.sem_inc(passed, 1)

        order = ["b1", "b3", "b6", "b8"]

        def fill_no(ph, b, name):
            per = 4 if ph["soft"] else 2
            return b * per + order.index(name)

        @block.tensor
        def _(pe):
            def fill(ph, b, name):
                if not (isinstance(b, int) and b == 0 and name == "b1"):
                    pe.wait_ge(ph["emptied"], fill_no(ph, b, name))

            def front_turn(ph, b):
                pe.wait_ge(ph["xn_in"], b + 1)
                for t in range(T):
                    ins = nc.tensor.transpose(psum[0][:, t * P:(t + 1) * P], xn[:, t, :], ident[:, :])
                ins.then_inc(ph["turn_done"], 1)

            def front_v(ph, b):
                pe.wait_ge(ph["ht_in"], b + 1)
                if not (isinstance(b, int) and b == 0):
                    pe.wait_ge(ph["v_out"], b)
                for t in range(T):
                    ins = nc.tensor.matmul(psum[1][:, t * P:(t + 1) * P], ht[:, t * P:(t + 1) * P], w_v[ph["w"]][:, :],
                                           start=(t == 0), stop=True, skip_group_check=True)
                ins.then_inc(ph["v_done"], 1)

            def front_qk(ph, b):
                if not (isinstance(b, int) and b == 0):
                    pe.wait_ge(ph["qk_out" if ph["soft"] else "full_in"], b)
                for k in range(2):
                    ins = nc.tensor.matmul(psum[2][:, k * 256:(k + 1) * 256], w_qk[ph["w"]][:, k, :], ht[:, :],
                                           start=(k == 0), stop=True, skip_group_check=True)
                ins.then_inc(ph["qk_done"], 1)

            def front_spread(ph, b, buf):
                pe.wait_ge(ph["qk_out"], b + 1)
                for k in range(2):
                    for g in range(G):
                        n = 2 * k + g // 2
                        if g % 2 == 0 and n in (0, 3) and not (isinstance(b, int) and b == 0):
                            if n == 0:
                                pe.wait_ge(ph["act_spread"], b * 3)
                            else:
                                pe.wait_ge(ph["dve_spread"], b)
                        bank = (psum[3:] + [bank_pv])[n]
                        for part, src in enumerate((qk_hi, qk_lo)):
                            ins = nc.tensor.matmul(bank[:, g % 2 * 256:(g % 2 + 1) * 256],
                                                   sel[:, k, part, g, :, :, :].rearrange("p a b c -> p (a b c)"),
                                                   src[:, buf, k, :], start=(g % 2 == 0 and part == 0),
                                                   stop=(part == 1), skip_group_check=True)
                        if g % 2:
                            ins.then_inc(ph["spread_done"], 1)

            def front_step(ph, b, buf, first=False, last=False):
                front_v(ph, b)
                front_qk(ph, b)
                if not last:
                    front_turn(ph, b + 1)
                if not first:
                    front_spread(ph, b - 1, 1 - buf)

            def front(ph):
                front_turn(ph, 0)
                front_step(ph, 0, 0, first=True)
                with pe.Fori(1, B - 1, 2) as b:
                    front_step(ph, b, 1)
                    front_step(ph, b + 1, 0)
                front_step(ph, B - 1, 1, last=True)
                front_spread(ph, B - 1, 1)
                pe.wait_ge(ph["act_spread"], 3 * B)
                pe.wait_ge(ph["dve_spread"], B)

            def back_turn(ph, b):
                pe.wait_ge(ph["cx_in"], b + 1)
                fill(ph, b, "b1")
                for t in range(T):
                    ins = nc.tensor.transpose(mx[:, t * P:(t + 1) * P], cx[:, t, :], ident[:, :])
                ins.then_inc(ph["filled"], 1)

            def back_wo(ph, b):
                fill(ph, b, "b3")
                for t in range(T):
                    ins = nc.tensor.matmul(mx[:, t * P:(t + 1) * P], cxt[:, t * P:(t + 1) * P], w_o[ph["w"]][:, :],
                                           start=(t == 0), stop=True, skip_group_check=True)
                ins.then_inc(ph["filled"], 1)

            def back_h2(ph, b):
                pe.wait_ge(ph["n2_in"], b + 1)
                fill(ph, b, "b6")
                for t in range(T):
                    ins = nc.tensor.transpose(mx[:, t * P:(t + 1) * P], n2[:, t, :], ident[:, :])
                ins.then_inc(ph["filled"], 1)

            def back_gate(ph, b):
                fill(ph, b, "b8")
                for t in range(T):
                    ins = nc.tensor.matmul(mx[:, t * E:(t + 1) * E], h2t[:, t * P:(t + 1) * P], gw[:, :],
                                           start=(t == 0), stop=True, skip_group_check=True)
                ins.then_inc(ph["filled"], 1)

            def natural(ph, b, g):
                if not (isinstance(b, int) and b == 0 and g == 0):
                    pe.wait_ge(ph["negm_in"], b * S + g)
                pe.wait_ge(ph["qk_loaded"][g // 2], LOADS * (b + 1))
                for c in range(2):
                    nc.tensor.matmul(banks_n[:, c, :], identb[:, :], maskb[:, :, :].rearrange("p a b -> p (a b)"),
                                     start=True, stop=False, skip_group_check=True)
                for j in range(GH):
                    for c, (tq, tk) in enumerate(((0, 0), (1, 1), (1, 0))):
                        ins = nc.tensor.matmul(banks_n[:, c, j * P:(j + 1) * P], qst[:, g, j, tq * P:(tq + 1) * P],
                                               kst[:, g, tk * P:(tk + 1) * P],
                                               start=(c == 2 and j == 0), stop=True, skip_group_check=True)
                ins.then_inc(ph["scored"], 1)

            def turned(ph, b, g):
                if ph["soft"]:
                    pe.wait_ge(ph["negm_in"], b * S + g + 1)
                else:
                    pe.wait_ge(ph["qk_loaded"][g // 2], LOADS * (b + 1))
                banks, free = (banks_t, 1) if ph["soft"] or g % 2 else (banks_n, 2)
                if not ph["soft"]:
                    free = 2
                if not (isinstance(b, int) and b == 0 and g < free):
                    pe.wait_ge(ph["exped"], b * S + g + 1 - free)
                for c, (tk, tq) in enumerate(((0, 0), (1, 1), (0, 1))):
                    ins = nc.tensor.matmul(banks[:, c, :], kst[:, g, tk * P:(tk + 1) * P],
                                           qst[:, g, :, tq * P:(tq + 1) * P],
                                           start=True, stop=not ph["soft"], skip_group_check=True)
                    for j in range(GH if ph["soft"] else 0):
                        ins = nc.tensor.matmul(banks_t[:, c, j * P:(j + 1) * P],
                                               negm[:, g % 2, tq, j:j + 1].to_broadcast([P, P]), ident16[:, :],
                                               start=False, stop=True, skip_group_check=True)
                ins.then_inc(ph["turned"], 1)

            def values(ph, b, g):
                pe.wait_ge(ph["v_loaded"][g // 2], 16 * (b + 1))
                pe.wait_ge(ph["p_lo_in"], b * S + g + 1)
                if g % 2 == 0 and not (isinstance(b, int) and b == 0 and g == 0):
                    pe.wait_ge(ph["pv_out"], 2 * b + g // 2)
                for j in range(GH):
                    h = GH * g + j
                    for tq, blocks in enumerate((((0, 0),), ((0, 2), (1, 1)))):
                        o = (tq * (H // 2) + h % (H // 2)) * VC
                        todo = [(src, tk, c) for tk, c in blocks for src in (p_hi, p_lo)]
                        for i, (src, tk, c) in enumerate(todo):
                            ins = nc.tensor.matmul(bank_pv[:, o:o + VC], src[:, g % 2, c, j, :],
                                                   v_hl[:, tk, h, :], start=(i == 0), stop=(i == len(todo) - 1),
                                                   skip_group_check=True)
                ins.then_inc(ph["pv_done"], 1)

            def next_natural(ph, b, g, last):
                if ph["soft"] and g + 1 < S:
                    natural(ph, b, g + 1)
                elif ph["soft"] and not last:
                    natural(ph, b + 1, 0)

            def iteration(ph, b, place=2, last=False):
                for g in range(S):
                    next_natural(ph, b, g, last)
                    if ph["soft"] and g == 2 and place > 1:
                        back_h2(ph, b - 2)
                    if g == 3 and place > 0:
                        back_turn(ph, b - 1)
                    turned(ph, b, g)
                    if g < 2 and place > 0:
                        values(ph, b - 1, g + 2)
                    if g >= 2:
                        values(ph, b, g - 2)
                    if ph["soft"] and g == 2 and place > 1:
                        back_gate(ph, b - 2)
                    if g == 3 and place > 0:
                        back_wo(ph, b - 1)

            def attention(ph):
                front(ph)
                if ph["soft"]:
                    natural(ph, 0, 0)
                iteration(ph, 0, place=0)
                iteration(ph, 1, place=1)
                with pe.Fori(2, B - 1) as b:
                    iteration(ph, b)
                iteration(ph, B - 1, last=True)
                values(ph, B - 1, S - 2)
                values(ph, B - 1, S - 1)
                if ph["soft"]:
                    back_h2(ph, B - 2)
                    back_gate(ph, B - 2)
                back_turn(ph, B - 1)
                back_wo(ph, B - 1)
                if ph["soft"]:
                    back_h2(ph, B - 1)
                    back_gate(ph, B - 1)

            def experts(m):
                K = E * HC

                def down(c, k):
                    e, hc = divmod(k, HC)
                    pe.wait_ge(m["hid_in"], c * K + k + 1)
                    if hc == 0 and not (isinstance(c, int) and c == 0 and e < 2):
                        pe.wait_ge(m["added"], c * E + e - 1)
                    for t in range(CH):
                        ins = nc.tensor.matmul(psum[4 + e % 2][:, t * P:(t + 1) * P],
                                               hid[:, k % 2, t * P:(t + 1) * P], w3s[:, e, hc, :],
                                               start=(hc == 0 and t == 0), stop=(hc == HC - 1), skip_group_check=True)
                    ins.then_inc(m["down_done"], 1)

                def chunk(c, first=False):
                    for k in range(K):
                        e, hc = divmod(k, HC)
                        if not (first and k < 2):
                            pe.wait_ge(m["hid_in"], c * K + k - 1)
                        for w in range(2):
                            ins = nc.tensor.matmul(psum[2 * (k % 2) + w][:, :], w12[:, e, w, hc * P:(hc + 1) * P],
                                                   h2t_all[:, bass.ds(c * CH, CH), :].rearrange("p a b -> p (a b)"),
                                                   start=True, stop=True)
                        ins.then_inc(m["up_done"], 1)
                        if k:
                            down(c, k - 1)
                        elif not first:
                            down(c - 1, K - 1)
                chunk(0, first=True)
                with pe.Fori(1, NT // CH) as c:
                    chunk(c)
                down(NT // CH - 1, K - 1)

            pe.wait_ge(w_in, weights_in)
            pe.wait_ge(consts, 1)
            for n, ph in enumerate(phases):
                attention(ph)
                if ph["soft"]:
                    pe.wait_ge(ph["h2_in"], B)
                    pe.wait_ge(w_moe, moe_in)
                    experts(mixtures[n // 2])

        @block.scalar
        def _(sc):
            def spread_out(ph, b):
                for n, (dst, half_of) in enumerate(((q_all, 0), (q_all, 1), (k_all, 0))):
                    sc.wait_ge(ph["spread_done"], 4 * b + n + 1)
                    nc.scalar.copy(dst[:, b, 2 * half_of:2 * half_of + 2, :].rearrange("p a b -> p (a b)"),
                                   psum[3 + n][:, :]).then_inc(ph["act_spread"], 1)

            def qk_high(ph, b, buf):
                sc.wait_ge(ph["qk_done"], b + 1)
                hi = qk_hi[:, buf, :, :].rearrange("p a b -> p (a b)")
                if ph["soft"]:
                    nc.scalar.copy(hi, psum[2][:, :]).then_inc(ph["hi_in"], 1)
                else:
                    if not (isinstance(b, int) and b == 0):
                        sc.wait_ge(ph["qk_out"], b)
                    nc.scalar.activation(qk_f[:, :, :].rearrange("p a b -> p (a b)"), psum[2][:, :], ACT.Exp)\
                        .then_inc(ph["exp_in"], 1)
                    sc.wait_ge(ph["full_in"], b + 1)
                    nc.scalar.copy(hi, qk_f[:, :, :].rearrange("p a b -> p (a b)")).then_inc(ph["hi_in"], 1)

            def v_high(ph, b):
                sc.wait_ge(ph["v_done"], b + 1)
                nc.scalar.copy(v_all[:, b, :, :, 0:HD], psum[1][:, 0:T * P].rearrange("p (t h d) -> p t h d", t=T, h=H))\
                    .then_inc(ph["v_hi"], 1)

            def front_step(ph, b, buf, first=False):
                v_high(ph, b)
                qk_high(ph, b, buf)
                if not first:
                    spread_out(ph, b - 1)

            def front(ph):
                front_step(ph, 0, 0, first=True)
                with sc.Fori(1, B - 1, 2) as b:
                    front_step(ph, b, 1)
                    front_step(ph, b + 1, 0)
                front_step(ph, B - 1, 1)
                spread_out(ph, B - 1)

            def exps(ph, b, g):
                sc.wait_ge(ph["turned"], b * S + g + 1)
                flat = "p a b c -> p (a b c)"
                if ph["soft"]:
                    if not (isinstance(b, int) and b == 0 and g < 2):
                        sc.wait_ge(ph["p_lo_in"], b * S + g - 1)
                    nc.scalar.activation(pf[:, g % 2, :, :, :].rearrange(flat),
                                         banks_t[:, :, :].rearrange("p a b -> p (a b)"), ACT.Exp,
                                         scale=HD ** -0.5).then_inc(ph["exped"], 1)
                else:
                    if not (isinstance(b, int) and b == 0 and g < 2):
                        sc.wait_ge(ph["pv_done"], b * S + g - 1)
                    nc.scalar.copy(p_hi[:, g % 2, :, :, :].rearrange(flat),
                                   (banks_t if g % 2 else banks_n)[:, :, :].rearrange("p a b -> p (a b)")).then_inc(ph["p_hi_in"], 1)

            def p_high(ph, b, g):
                if not ph["soft"]:
                    return
                sc.wait_ge(ph["masked"], b * S + g + 1)
                if not (isinstance(b, int) and b == 0 and g < 2):
                    sc.wait_ge(ph["pv_done"], b * S + g - 1)
                flat = "p a b c -> p (a b c)"
                nc.scalar.copy(p_hi[:, g % 2, :, :, :].rearrange(flat), pf[:, g % 2, :, :, :].rearrange(flat))\
                    .then_inc(ph["p_hi_in"], 1)

            def pv_read(ph, b, hf):
                sc.wait_ge(ph["pv_done"], b * S + 2 * (hf + 1))
                nc.scalar.copy(pv_sb[:, :, hf * 8:(hf + 1) * 8, :],
                               bank_pv[:, 0:T * 8 * VC].rearrange("p (t h d) -> p t h d", t=T, h=8))\
                    .then_inc(ph["pv_out"], 1)

            def ctx_turned(ph, b):
                sc.wait_ge(ph["filled"], fill_no(ph, b, "b1") + 1)
                nc.scalar.copy(cxt[:, :], mx[:, 0:T * P]).then_inc(ph["emptied"], 1)

            def h2_turned(ph, b):
                sc.wait_ge(ph["filled"], fill_no(ph, b, "b6") + 1)
                nc.scalar.activation(h2t_all[:, bass.ds(2 * b, 2), :].rearrange("p a b -> p (a b)"), mx[:, 0:T * P],
                                     ACT.Identity, scale=ln[:, 2:3], bias=ln[:, 3:4]).then_inc(ph["h2_in"], 1)
                nc.scalar.activation(h2t[:, :], mx[:, 0:T * P], ACT.Identity,
                                     scale=ln[:, 2:3], bias=ln[:, 3:4]).then_inc(ph["emptied"], 1)

            def gates_out(ph, b):
                sc.wait_ge(ph["filled"], fill_no(ph, b, "b8") + 1)
                nc.scalar.copy(gates[:, bass.ds(2 * b, 2), :].rearrange("p a b -> p (a b)"), mx[:, 0:T * E])\
                    .then_inc(ph["emptied"], 1)

            def iteration(ph, b, place=2, last=False):
                for g in range(S):
                    if ph["soft"] and g == 2 and place > 1:
                        h2_turned(ph, b - 2)
                    if ph["soft"] and g == 3 and place > 1:
                        gates_out(ph, b - 2)
                    if g == 3 and place > 0:
                        ctx_turned(ph, b - 1)
                    exps(ph, b, g)
                    if g:
                        p_high(ph, b, g - 1)
                    elif place > 0:
                        p_high(ph, b - 1, S - 1)
                    if g == 1 and place > 0:
                        pv_read(ph, b - 1, 1)
                    if g == 3:
                        pv_read(ph, b, 0)

            def attention(ph):
                front(ph)
                iteration(ph, 0, place=0)
                iteration(ph, 1, place=1)
                with sc.Fori(2, B) as b:
                    iteration(ph, b)
                p_high(ph, B - 1, S - 1)
                if ph["soft"]:
                    h2_turned(ph, B - 2)
                    gates_out(ph, B - 2)
                pv_read(ph, B - 1, 1)
                ctx_turned(ph, B - 1)
                if ph["soft"]:
                    h2_turned(ph, B - 1)
                    gates_out(ph, B - 1)

            def experts(m):
                K = E * HC
                sc.wait_ge(m["route_in"], 1)
                nc.scalar.activation(prob[:, :, 0], prob[:, :, 0], ACT.Exp).then_inc(m["e_in"], 1)

                def chunk(c, first=False):
                    for k in range(K):
                        sc.wait_ge(m["up_done"], c * K + k + 1)
                        if not (first and k < 2):
                            sc.wait_ge(m["hid_in"], c * K + k - 1)
                        nc.scalar.activation(act_s[:, k % 2, :], psum[2 * (k % 2)][:, :], ACT.Silu)\
                            .then_inc(m["silu_in"], 1)
                chunk(0, first=True)
                with sc.Fori(1, NT // CH) as c:
                    chunk(c)

            sc.wait_ge(w_in, weights_in)
            for n, ph in enumerate(phases):
                attention(ph)
                if ph["soft"]:
                    experts(mixtures[n // 2])

        @block.vector
        def _(ve):
            def front_stats(ph, part):
                for n in STATS[part]:
                    ins = nc.vector.bn_stats(st[:, n, :], x_all[:, n // T, n % T, :])
                ins.then_inc(ph["stats"], 1)
                ve.wait_ge(ph["stats"], 2 * part + 1)
                for n in STATS[part]:
                    ins = nc.vector.bn_aggr(mv[:, n, :], st[:, n, :])
                ins.then_inc(ph["stats"], 1)

            def front_norm(ph, b):
                def of(array, t):
                    return array[:, bass.ds(T * b + t, 1)]
                for t in range(T):
                    ins = nc.vector.tensor_scalar(xn[:, t, :], x_all[:, b, t, :], of(mv[:, :, 0], t),
                                                  of(rs[:, 5 if ph["soft"] else 1, :], t), ALU.subtract, ALU.mult)
                ins.then_inc(ph["xn_in"], 1)

            def back_y(ph, b):
                def of(array, t):
                    return array[:, bass.ds(T * b + t, 1)]
                for t in range(T):
                    ins = nc.vector.tensor_scalar(yb[:, t, :], x_all[:, b, t, :], of(mv[:, :, 0], t),
                                                  of(rs[:, 1, :], t), ALU.subtract, ALU.mult)
                ins.then_inc(ph["y_in"], 1)

            def front_ht(ph, b):
                ve.wait_ge(ph["turn_done"], b + 1)
                if ph["soft"]:
                    nc.vector.tensor_scalar(ht[:, :], psum[0][:, 0:T * P], ln[:, 0:1], ln[:, 1:2], ALU.mult, ALU.add)\
                        .then_inc(ph["ht_in"], 1)
                else:
                    nc.vector.tensor_copy(ht[:, :], psum[0][:, 0:T * P]).then_inc(ph["ht_in"], 1)

            def qk_elu(ph, b):
                if ph["soft"]:
                    return
                flat = qk_f[:, :, :].rearrange("p a b -> p (a b)")
                ve.wait_ge(ph["exp_in"], b + 1)
                nc.vector.tensor_scalar(flat, flat, 1.0, None, ALU.min).then_inc(ph["neg_in"], 1)
                ve.wait_ge(ph["neg_in"], b + 1)
                nc.vector.scalar_tensor_tensor(flat, psum[2][:, :], 0.0, flat, ALU.max, ALU.add)\
                    .then_inc(ph["full_in"], 1)

            def qk_low(ph, b, buf):
                ve.wait_ge(ph["hi_in"], b + 1)
                nc.vector.tensor_tensor(qk_lo[:, buf, :, :].rearrange("p a b -> p (a b)"),
                                        psum[2][:, :] if ph["soft"] else qk_f[:, :, :].rearrange("p a b -> p (a b)"),
                                        qk_hi[:, buf, :, :].rearrange("p a b -> p (a b)"), ALU.subtract)\
                    .then_inc(ph["qk_out"], 1)

            def spread_out(ph, b):
                ve.wait_ge(ph["spread_done"], 4 * b + 4)
                nc.vector.tensor_copy(k_all[:, b, 2:4, :].rearrange("p a b -> p (a b)"), bank_pv[:, :])\
                    .then_inc(ph["dve_spread"], 1)

            def v_low(ph, b):
                ve.wait_ge(ph["v_hi"], b + 1)
                nc.vector.tensor_tensor(v_all[:, b, :, :, HD + 1:VC],
                                        psum[1][:, 0:T * P].rearrange("p (t h d) -> p t h d", t=T, h=H),
                                        v_all[:, b, :, :, 0:HD], ALU.subtract).then_inc(ph["v_out"], 1)

            def front_step(ph, b, buf, first=False, last=False, before_last=False):
                v_low(ph, b)
                if not last:
                    front_ht(ph, b + 1)
                if not (last or before_last):
                    front_norm(ph, b + 2)
                qk_elu(ph, b)
                qk_low(ph, b, buf)
                if not first:
                    spread_out(ph, b - 1)

            def front(ph):
                if ph is phases[0]:
                    ve.wait_ge(x_in[0], 16)
                front_stats(ph, 0)
                ve.wait_ge(ph["rstd"], 1)
                front_norm(ph, 0)
                front_ht(ph, 0)
                front_norm(ph, 1)
                front_step(ph, 0, 0, first=True)
                if ph is phases[0]:
                    ve.wait_ge(x_in[1], 16)
                front_stats(ph, 1)
                ve.wait_ge(ph["rstd"], 2)
                with ve.Fori(1, B - 3, 2) as b:
                    front_step(ph, b, 1)
                    front_step(ph, b + 1, 0)
                front_step(ph, B - 3, 1)
                front_step(ph, B - 2, 0, before_last=True)
                front_step(ph, B - 1, 1, last=True)
                spread_out(ph, B - 1)

            def maxima(ph, b, g):
                if not ph["soft"]:
                    return
                ve.wait_ge(ph["scored"], b * S + g + 1)
                nc.vector.tensor_reduce(negm[:, g % 2, 0, :], banks_n[:, 0, :].rearrange("p (h k) -> p h k", h=GH),
                                        AX.X, ALU.max, negate=True)
                nc.vector.tensor_reduce(negm[:, g % 2, 1, :],
                                        banks_n[:, 1:3, :].rearrange("p c (h k) -> p h c k", h=GH),
                                        AX.XY, ALU.max, negate=True).then_inc(ph["negm_in"], 1)

            def p_low(ph, b, g):
                ve.wait_ge(ph["p_hi_in"], b * S + g + 1)
                flat = "p a b c -> p (a b c)"
                lo, hi = p_lo[:, g % 2, :, :, :].rearrange(flat), p_hi[:, g % 2, :, :, :].rearrange(flat)
                if ph["soft"]:
                    nc.vector.tensor_tensor(lo, pf[:, g % 2, :, :, :].rearrange(flat), hi, ALU.subtract)\
                        .then_inc(ph["p_lo_in"], 1)
                else:
                    nc.vector.tensor_tensor(lo, (banks_t if g % 2 else banks_n)[:, :, :].rearrange("p a b -> p (a b)"), hi, ALU.subtract)\
                        .then_inc(ph["exped"], 1)

            def back_context(ph, b):
                c = Chain(ve, ph["cv_back"], b * ph["back_links"])
                ve.wait_ge(ph["pv_out"], 2 * b + 2)
                if ph["soft"]:
                    c.link(nc.vector.tensor_tensor(num[:, :, :, :], pv_sb[:, :, :, 0:HD], pv_sb[:, :, :, HD + 1:VC],
                                                   ALU.add))
                    c.link(nc.vector.reciprocal(rden[:, :, :], pv_sb[:, :, :, HD]))
                else:
                    c.link(nc.vector.tensor_scalar(rden[:, :, :], pv_sb[:, :, :, HD], 1e-6, None, ALU.max))
                    nc.vector.tensor_tensor(num[:, :, :, :], pv_sb[:, :, :, 0:HD], pv_sb[:, :, :, HD + 1:VC], ALU.add)
                    c.link(nc.vector.reciprocal(rden[:, :, :], rden[:, :, :]))
                nc.vector.tensor_tensor(cx[:, :, :].rearrange("p t (h d) -> p t h d", h=H), num[:, :, :, :],
                                        rden[:, :, :].unsqueeze(3).to_broadcast([P, T, H, HD]), ALU.mult)\
                    .then_inc(ph["cx_in"], 1)

            def back_add(ph, b):
                ve.wait_ge(ph["filled"], fill_no(ph, b, "b3") + 1)
                src = mx[:, 0:T * P].rearrange("p (t d) -> p t d", t=T)
                if not ph["soft"]:
                    nc.vector.tensor_tensor(x_all[:, b, :, :], src, x_all[:, b, :, :], ALU.add)\
                        .then_inc(ph["emptied"], 1)
                    return
                c = Chain(ve, ph["cv_back"], b * ph["back_links"])
                c.n = 2
                ve.wait_ge(ph["y_bias"], b + 1)
                nc.vector.tensor_tensor(y2[:, :, :], src, yb[:, :, :], ALU.add).then_inc(ph["emptied"], 1)
                ve.wait_ge(ph["emptied"], fill_no(ph, b, "b3") + 1)
                for t in range(T):
                    c.link(nc.vector.bn_stats(st2[:, t, :], y2[:, t, :]))
                apart(ve)
                nc.vector.bn_aggr(mv2[:, 0, :], st2[:, 0, :])
                nc.vector.bn_aggr(mv2[:, 1, :], st2[:, 1, :]).then_inc(ph["stats2"], 1)
                nc.vector.scalar_tensor_tensor(x_all[:, b, :, :], y2[:, :, :], 0.5, x_all[:, b, :, :],
                                               ALU.mult, ALU.add).then_inc(ph["x_in"], 1)
                c.end(ph["back_links"])

            def back_norm(ph, b):
                ve.wait_ge(ph["rstd2"], b + 1)
                for t in range(T):
                    ins = nc.vector.tensor_scalar(n2[:, t, :], y2[:, t, :], mv2[:, t, 0:1],
                                                  rs2[:, 1, t:t + 1], ALU.subtract, ALU.mult)
                ins.then_inc(ph["n2_in"], 1)

            def iteration(ph, b, place=2, last=False):
                for g in range(S):
                    if g + 1 < S:
                        maxima(ph, b, g + 1)
                    elif not last:
                        maxima(ph, b + 1, 0)
                    if g == 0 and place > 1:
                        back_add(ph, b - 2)
                    if ph["soft"] and g == 1 and place > 1:
                        back_norm(ph, b - 2)
                    if ph["soft"] and g == 1 and place > 0:
                        back_y(ph, b - 1)
                    if g == 2 and place > 0:
                        back_context(ph, b - 1)
                    if not ph["soft"]:
                        p_low(ph, b, g)
                    elif g:
                        p_low(ph, b, g - 1)
                    elif place > 0:
                        p_low(ph, b - 1, S - 1)

            def attention(ph):
                front(ph)
                maxima(ph, 0, 0)
                iteration(ph, 0, place=0)
                iteration(ph, 1, place=1)
                with ve.Fori(2, B - 1) as b:
                    iteration(ph, b)
                iteration(ph, B - 1, last=True)
                if ph["soft"]:
                    p_low(ph, B - 1, S - 1)
                back_add(ph, B - 2)
                if ph["soft"]:
                    back_norm(ph, B - 2)
                    back_y(ph, B - 1)
                back_context(ph, B - 1)
                back_add(ph, B - 1)
                if ph["soft"]:
                    back_norm(ph, B - 1)

            def experts(ph, m):
                c = Chain(ve, m["chain"], 0)
                ve.wait_ge(ph["emptied"], fill_no(ph, B - 1, "b8") + 1)
                ve.wait_ge(ph["x_in"], B)
                for n in range(NT):
                    ins = nc.vector.max(top[:, n, :], gates[:, n, :])
                c.link(ins)
                for n in range(NT):
                    ins = nc.vector.max_index(topi[:, n, :], top[:, n, :], gates[:, n, :])
                nc.vector.tensor_tensor(prob[:, :, 0], top[:, :, 1], top[:, :, 0], ALU.subtract)\
                    .then_inc(m["route_in"], 1)
                c.link(ins)
                c.link(nc.vector.tensor_copy(topf[:, :, :], topi[:, :, 0:2]))
                ve.wait_ge(m["e_in"], 1)
                c.link(nc.vector.tensor_scalar(prob[:, :, 1], prob[:, :, 0], 1.0, None, ALU.add))
                c.link(nc.vector.reciprocal(prob[:, :, 1], prob[:, :, 1]))
                c.link(nc.vector.tensor_scalar(prob[:, :, 1], prob[:, :, 1], 0.5, None, ALU.mult))
                c.link(nc.vector.tensor_tensor(prob[:, :, 2], prob[:, :, 0], prob[:, :, 1], ALU.mult))
                for k, dst in ((0, route), (1, onehot)):
                    c.link(nc.vector.tensor_tensor(dst[:, :, :], iota_e[:, :].unsqueeze(1).to_broadcast([P, NT, E]),
                                                   topf[:, :, k:k + 1].to_broadcast([P, NT, E]), ALU.is_equal))
                    c.link(nc.vector.tensor_tensor(dst[:, :, :], dst[:, :, :],
                                                   prob[:, :, k + 1:k + 2].to_broadcast([P, NT, E]), ALU.mult))
                c.link(nc.vector.tensor_tensor(route[:, :, :], route[:, :, :], onehot[:, :, :], ALU.add))
                K = E * HC

                def product(cc, k):
                    ve.wait_ge(m["silu_in"], cc * K + k + 1)
                    if not (isinstance(cc, int) and cc == 0 and k < 2):
                        ve.wait_ge(m["down_done"], cc * K + k - 1)
                    nc.vector.tensor_tensor(hid[:, k % 2, :], psum[2 * (k % 2) + 1][:, :], act_s[:, k % 2, :],
                                            ALU.mult).then_inc(m["hid_in"], 1)

                def add(cc, e):
                    ve.wait_ge(m["down_done"], cc * K + HC * (e + 1))
                    if not (isinstance(cc, int) and cc == 0 and e == 0):
                        ve.wait_ge(m["added"], cc * E + e)
                    for t in range(CH):
                        y = x_all[:, :, :, :].rearrange("p b t d -> p (b t) d")[:, bass.ds(cc * CH + t, 1), :]\
                            .rearrange("p a d -> p (a d)")
                        r = route[:, bass.ds(cc * CH + t, 1), e:e + 1].rearrange("p a b -> p (a b)")
                        ins = nc.vector.scalar_tensor_tensor(y, psum[4 + e % 2][:, t * P:(t + 1) * P], r, y,
                                                             ALU.mult, ALU.add)
                    ins.then_inc(m["added"], 1)

                def chunk(cc, first=False):
                    for k in range(K):
                        product(cc, k)
                        if k >= 2 and k % 2 == 0:
                            add(cc, k // 2 - 1)
                        if k == 0 and not first:
                            add(cc - 1, E - 1)
                chunk(0, first=True)
                with ve.Fori(1, NT // CH) as cc:
                    chunk(cc)
                add(NT // CH - 1, E - 1)
                ve.wait_ge(m["added"], NT // CH * E)

            ve.wait_ge(w_in, weights_in)
            ve.wait_ge(consts, 1)
            for n, ph in enumerate(phases):
                attention(ph)
                if not ph["soft"]:
                    ve.wait_ge(ph["emptied"], fill_no(ph, B - 1, "b3") + 1)
                if ph["soft"]:
                    experts(ph, mixtures[n // 2])

        @block.gpsimd
        def _(gp):
            pools = sem("pools")
            c = Chain(gp, pools, 0)

            def diag(t, fill=1.0):
                c.link(nc.gpsimd.memset(t, 0.0))
                c.link(nc.gpsimd.affine_select(out=t, in_=t, pattern=[[-1, P]], compare_op=ALU.not_equal, fill=fill,
                                               base=0, channel_multiplier=1))
            diag(ident[:, :])
            diag(ident16[:, :])
            diag(identb[:, :])
            c.link(nc.gpsimd.memset(maskb[:, :, :], 0.0))
            c.link(nc.gpsimd.affine_select(out=maskb[:, :, :], in_=maskb[:, :, :], pattern=[[0, GH], [-1, P]],
                                           compare_op=ALU.is_ge, fill=BIG, base=0, channel_multiplier=1))
            c.link(nc.gpsimd.memset(sel[:, :, :, :, :, :, :], 0.0))
            for k, rows in enumerate((((0, 1), (2,)), ((0, 2), (1,)))):
                for part, blocks in enumerate(rows):
                    for r in blocks:
                        at = sel[:, k, part, :, :, r, :]
                        c.link(nc.gpsimd.affine_select(out=at, in_=at, pattern=[[-32, G], [-8, 4], [-1, HD]],
                                                       compare_op=ALU.not_equal, fill=1.0, base=0,
                                                       channel_multiplier=1))
            c.link(nc.gpsimd.memset(v_all[:, :, :, :, HD:HD + 1].rearrange("p a b c d -> p (a b c) d"), 1.0))
            c.link(nc.gpsimd.memset(qst[:, :, :, :].rearrange("p a b c -> p (a b c)"), 0.0))
            c.link(nc.gpsimd.memset(half[:, :], -0.5))
            nc.gpsimd.iota(iota_e[:, :], pattern=[[1, E]], base=0, channel_multiplier=0,
                           allow_small_or_imprecise_dtypes=True).then_inc(consts, 1)

            def front_rstd(ph, part):
                s = slice(STATS[part][0], STATS[part][-1] + 1)
                c = Chain(gp, ph["cp_front"], part * (6 if ph["soft"] else 1))
                gp.wait_ge(ph["stats"], 2 * part + 2)
                c.link(nc.gpsimd.tensor_scalar(rs[:, 0, s], mv[:, s, 1], EPS, None, ALU.add))
                if not ph["soft"]:
                    nc.gpsimd.tensor_tensor(rs[:, 1, s], rs[:, 0, s], half[:, s], ALU.pow).then_inc(ph["rstd"], 1)
                    return
                c.link(nc.gpsimd.tensor_tensor(rs[:, 1, s], rs[:, 0, s], half[:, s], ALU.pow))
                c.link(nc.gpsimd.tensor_tensor(rs[:, 2, s], mv[:, s, 1], rs[:, 1, s], ALU.mult))
                c.link(nc.gpsimd.tensor_tensor(rs[:, 2, s], rs[:, 2, s], rs[:, 1, s], ALU.mult))
                c.link(nc.gpsimd.tensor_scalar(rs[:, 3, s], rs[:, 2, s], EPS, None, ALU.add))
                c.link(nc.gpsimd.tensor_tensor(rs[:, 4, s], rs[:, 3, s], half[:, s], ALU.pow))
                nc.gpsimd.tensor_tensor(rs[:, 5, s], rs[:, 4, s], rs[:, 1, s], ALU.mult).then_inc(ph["rstd"], 1)

            def back_bias(ph, b):
                gp.wait_ge(ph["y_in"], b + 1)
                nc.gpsimd.tensor_tensor(yb[:, :, :], yb[:, :, :], bo_b[:, :].unsqueeze(1).to_broadcast([P, T, P]),
                                        ALU.add).then_inc(ph["y_bias"], 1)

            def back_rstd(ph, b):
                c = Chain(gp, ph["cp_back"], b)
                gp.wait_ge(ph["stats2"], b + 1)
                apart(gp)
                c.link(nc.gpsimd.tensor_scalar(rs2[:, 0, :], mv2[:, :, 1], EPS, None, ALU.add))
                nc.gpsimd.tensor_tensor(rs2[:, 1, :], rs2[:, 0, :], half[:, 0:T], ALU.pow).then_inc(ph["rstd2"], 1)

            def causal(ph, b, g):
                def select(src):
                    at = src[:, g % 2, 0:2, :, :].rearrange("p a b c -> p (a b c)")
                    return nc.gpsimd.affine_select(out=at, in_=at, pattern=[[0, 2 * GH], [1, P]],
                                                   compare_op=ALU.is_ge, fill=0.0, base=0, channel_multiplier=-1)
                gp.wait_ge(ph["exped"], b * S + g + 1)
                apart(gp)
                if ph["soft"]:
                    select(pf).then_inc(ph["masked"], 1)
                else:
                    select(p_hi)
                    select(p_lo).then_inc(ph["p_lo_in"], 1)

            def iteration(ph, b, place=2):
                for g in range(S):
                    causal(ph, b, g)
                    if ph["soft"] and g == 0 and place > 1:
                        back_rstd(ph, b - 2)
                    if ph["soft"] and g == 1 and place > 0:
                        back_bias(ph, b - 1)

            def attention(ph):
                front_rstd(ph, 0)
                front_rstd(ph, 1)
                iteration(ph, 0, place=0)
                iteration(ph, 1, place=1)
                with gp.Fori(2, B) as b:
                    iteration(ph, b)
                if ph["soft"]:
                    back_rstd(ph, B - 2)
                    back_bias(ph, B - 1)
                    back_rstd(ph, B - 1)

            gp.wait_ge(w_in, weights_in)
            for ph in phases:
                attention(ph)

        @block.sync
        def _(sy):
            for n, bs in enumerate((slice(0, STATS[0][-1] // T + 1), slice(STATS[0][-1] // T + 1, B))):
                sy.dma_start(x_all[:, bs, :, :], x.rearrange("b (t p) d -> p b t d", p=P)[:, bs]).then_inc(x_in[n], 16)
            n = 0
            for k, (q_, k_, v_, o_) in enumerate(((wq, wk, wv, wo), (Wq, Wk, Wv, Wo))):
                for dst, src in ((w_qk[k][:, 0, :], q_), (w_qk[k][:, 1, :], k_), (w_v[k][:, :], v_), (w_o[k][:, :], o_)):
                    sy.dma_start(dst, src).then_inc(w_in, 16)
                    n += 1
            for k, src in enumerate((ln1_s, ln1_b, ln2_s, ln2_b)):
                sy.dma_start(ln[:, k:k + 1], src.rearrange("(p a) -> p a", a=1)).then_inc(w_in, 16)
                n += 1
            sy.dma_start(bo_b[:, :], bo.unsqueeze(0).to_broadcast([P, P])).then_inc(w_in, 16)
            sy.dma_start(gw[:, :], gate_w).then_inc(w_in, 16)
            n += 2
            for e0 in (0, 4):
                for k, src in enumerate((w1, w2)):
                    sy.dma_start(w12[:, e0:e0 + 4, k, :], src[e0:e0 + 4].rearrange("e d h -> d e h"))\
                        .then_inc(w_moe, 16)
            for c in range(HC):
                for e0 in (0, 4):
                    sy.dma_start(w3s[:, e0:e0 + 4, c, :],
                                 w3[e0:e0 + 4, c * P:(c + 1) * P, :].rearrange("e h d -> h e d")).then_inc(w_moe, 16)
            assert n * 16 == weights_in, n

            def load_qk(ph, b, hf):
                gs = slice(2 * hf, 2 * hf + 2)
                for j in range(GH):
                    rows = slice(32 * j, 32 * (j + 1))
                    sy.dma_start(qst[rows, gs, j, :], q_all[rows, b, gs, :]).then_inc(ph["qk_loaded"][hf], 16)
                sy.dma_start(kst[:, gs, :], k_all[:, b, gs, :]).then_inc(ph["qk_loaded"][hf], 16)

            def load_v(ph, b, hf):
                heads = slice(8 * hf, 8 * (hf + 1))
                sy.dma_start(v_hl[:, :, heads, :], v_all[:, b, :, heads, :]).then_inc(ph["v_loaded"][hf], 16)

            def next_v(ph, b, hf):
                sy.wait_ge(ph["pv_done"], b * S + 2 * hf + 2)
                load_v(ph, b + 1, hf)

            def next_qk(ph, b, hf):
                sy.wait_ge(ph["turned"], b * S + 2 * hf + 2)
                load_qk(ph, b + 1, hf)

            def attention(ph):
                sy.wait_ge(ph["act_spread"], 3)
                sy.wait_ge(ph["dve_spread"], 1)
                sy.wait_ge(ph["v_out"], 1)
                for hf in range(2):
                    load_qk(ph, 0, hf)
                for hf in range(2):
                    load_v(ph, 0, hf)
                sy.wait_ge(ph["act_spread"], 3 * B)
                sy.wait_ge(ph["dve_spread"], B)
                sy.wait_ge(ph["v_out"], B)
                next_qk(ph, 0, 0)
                next_qk(ph, 0, 1)
                next_v(ph, 0, 0)
                with sy.Fori(1, B - 1) as b:
                    next_qk(ph, b, 0)
                    next_v(ph, b - 1, 1)
                    next_qk(ph, b, 1)
                    next_v(ph, b, 0)
                next_v(ph, B - 2, 1)

            sy.wait_ge(consts, 1)
            for ph in phases:
                attention(ph)
            sy.wait_ge(mixtures[1]["added"], NT // CH * E)
            sy.dma_start(out.rearrange("b (t p) d -> p b t d", p=P), x_all[:, :, :, :]).then_inc(outs, 16)
            sy.wait_ge(outs, 16)


_INS = ["L0_attn_x", "L0_attn_Wq", "L0_attn_Wk", "L0_attn_Wv", "L0_attn_Wo", "L0_ffn_ln1_scale", "L0_ffn_ln1_shift",
        "L0_ffn_wq", "L0_ffn_wk", "L0_ffn_wv", "L0_ffn_wo", "L0_ffn_bo", "L0_ffn_ln2_scale", "L0_ffn_ln2_shift",
        "L0_ffn_gate_w", "L0_ffn_w1", "L0_ffn_w2", "L0_ffn_w3"]


def kernel(**inputs):
    import numpy as np
    import concourse.bacc as bacc
    from concourse.bass_utils import run_bass_kernel_spmd

    nc = bacc.Bacc("TRN2", target_bir_lowering=False, num_devices=1)
    arrays, args = {}, []
    for name in _INS:
        a = np.asarray(inputs[name])
        if name.startswith("L0_attn_W"):
            a = a.T
        arrays[name] = np.ascontiguousarray(a)
        args.append(nc.dram_tensor(name, a.shape, F32, kind="ExternalInput").ap())
    args.append(nc.dram_tensor("out", inputs["L0_attn_x"].shape, F32, kind="ExternalOutput").ap())
    build(nc, *args)
    return run_bass_kernel_spmd(nc, [arrays], core_ids=[0]).results[0]["out"]
```

```python
from contextlib import ExitStack

import concourse.bass as bass
from concourse import mybir

F32 = mybir.dt.float32
F16 = mybir.dt.float16
BF16 = mybir.dt.bfloat16
U32 = mybir.dt.uint32
ALU = mybir.AluOpType
ACT = mybir.ActivationFunctionType
AX = mybir.AxisListType

P = 128
B = 16
T = 2
NT = B * T
H = 16
HD = P // H
G = 4
S = G
GH = H // G
LOADS = 16 * 5
VC = 2 * HD + 1
E = 8
HID = 256
HC = HID // P
CH = 4
EPS = 1e-5
STATS = (range(0, 6), range(6, 14), range(14, NT))
BIG = -1e30


class Chain:

    def __init__(self, eng, sem, base):
        self.eng, self.sem, self.base, self.n = eng, sem, base, 0

    def link(self, ins):
        ins.then_inc(self.sem, 1)
        self.n += 1
        self.eng.wait_ge(self.sem, self.base + self.n)

    def end(self, n):
        assert self.n == n, (self.n, n)


def tile_at(array, b):
    return array[:, b, :, :]


def build(nc, x, Wq, Wk, Wv, Wo, ln1_s, ln1_b, wq, wk, wv, wo, bo, ln2_s, ln2_b, gate_w, w1, w2, w3, out):
    ctx = ExitStack()

    def sb(name, shape, dt=F32):
        return ctx.enter_context(nc.sbuf_tensor(name, shape, dt))

    with ctx:
        x_all = sb("x_all", [P, B, T, P])
        yb = sb("yb", [P, T, P])
        y2 = sb("y2", [P, T, P])
        h2t_all = sb("h2t_all", [P, 2, NT, P], F16)
        gates = sb("gates", [P, NT, E])
        route = sb("route", [P, NT, E])
        top = sb("top", [P, NT, 8])
        topi = sb("topi", [P, NT, 8], U32)
        topf = sb("topf", [P, NT, 2])
        prob = sb("prob", [P, NT, 3])
        onehot = sb("onehot", [P, NT, E])
        w_qk = [sb(f"w_qk{n}", [P, 2, P]) for n in range(2)]
        w_v = [sb(f"w_v{n}", [P, P]) for n in range(2)]
        w_o = [sb(f"w_o{n}", [P, P]) for n in range(2)]
        ln = sb("ln", [P, 4])
        bo_b = sb("bo_b", [P, P])
        gw = sb("gw", [P, E])
        w12 = sb("w12", [P, E, 2, 2, HID], F16)
        w3s = sb("w3s", [P, 2, E, HC, P], F16)
        ident = sb("ident", [P, P])
        ident16 = sb("ident16", [P, P], F16)
        identb = sb("identb", [P, P], BF16)
        maskb = sb("maskb", [P, GH, P], BF16)
        sel = sb("sel", [P, 2, 2, G, 4, 4, HD], F16)
        iota_e = sb("iota_e", [P, E])
        half = sb("half", [P, NT])
        st = sb("st", [P, NT, 6])
        mv = sb("mv", [P, NT, 2])
        rs = sb("rs", [P, 6, NT])
        st2 = sb("st2", [P, T, 6])
        mv2 = sb("mv2", [P, T, 2])
        rs2 = sb("rs2", [P, 2, T])
        xn = sb("xn", [P, T, P])
        ht = sb("ht", [P, T * P])
        q_all = sb("q_all", [P, B, G, T * P], F16)
        k_all = sb("k_all", [P, B, G, T * P], F16)
        v_all = sb("v_all", [P, B, T, H, VC], F16)
        kst = sb("kst", [P, G, T * P], F16)
        qst = sb("qst", [P, G, GH, T * P], F16)
        v_hl = sb("v_hl", [P, T, H, VC], F16)
        negm = sb("negm", [P, 2, T, GH], F16)
        pf = sb("pf", [P, 2, 3, GH, P])
        p_hi = sb("p_hi", [P, 2, 3, GH, P], F16)
        p_lo = sb("p_lo", [P, 2, 3, GH, P], F16)
        pv_sb = sb("pv_sb", [P, T, H, VC])
        rden = sb("rden", [P, T, H])
        num = sb("num", [P, T, H, HD])
        cx = sb("cx", [P, T, P])
        cxt = sb("cxt", [P, T * P])
        n2 = sb("n2", [P, T, P])
        h2t = sb("h2t", [P, T * P])
        qk_hi, qk_lo = [a[:, :, :, :, :].rearrange("p a b c d -> p (a b c d)")[:, 0:2 * 2 * T * P]
                        .rearrange("p (n k m) -> p n k m", n=2, k=2) for a in (p_hi, p_lo)]
        qk_f = pf[:, :, :, :, :].rearrange("p a b c d -> p (a b c d)")[:, 0:2 * T * P]\
            .rearrange("p (k m) -> p k m", k=2)
        more = pf[:, :, :, :, :].rearrange("p a b c d -> p (a b c d)").bitcast(F16)\
            .rearrange("p (n a c d) -> p n a c d", n=4, a=3, c=GH)

        def parts_of(ph, g):
            if ph["soft"] or g < 2:
                return p_hi[:, g % 2, :, :, :], p_lo[:, g % 2, :, :, :]
            return more[:, g - 2, :, :, :], more[:, g, :, :, :]

        spare = pf[:, :, :, :, :].rearrange("p a b c d -> p (a b c d)")
        act_s = spare[:, 0:2 * CH * P].rearrange("p (a b) -> p a b", a=2)
        hid = spare[:, 2 * CH * P:4 * CH * P].rearrange("p (a b) -> p a b", a=2)
        hid_hi, hid_lo = [a[:, :, :, :, :].rearrange("p a b c d -> p (a b c d)")[:, 0:2 * CH * P]
                          .rearrange("p (a b) -> p a b", a=2) for a in (p_hi, p_lo)]
        stage = h2t_all[:, :, :, :].rearrange("p a b c -> p (a b c)").bitcast(F32)
        stage12 = stage.rearrange("p (e w h) -> p e w h", e=E, w=2)
        stage3 = stage[:, 0:E * HC * P].rearrange("p (e c d) -> p e c d", e=E, c=HC)

        banks_n = ctx.enter_context(nc.psum_tensor("banks_n", [P, 3, 512], F32))
        banks_t = ctx.enter_context(nc.psum_tensor("banks_t", [P, 3, 512], F32))
        bank_pv = ctx.enter_context(nc.psum_tensor("bank_pv", [P, 512], F32))
        mx = ctx.enter_context(nc.psum_tensor("bank_mx", [P, 512], F32))
        psum = [banks_n[:, n, :] for n in range(3)] + [banks_t[:, n, :] for n in range(3)]

        def sem(name):
            return ctx.enter_context(nc.semaphore(name))

        x_in, w_in, consts, outs, passed = [sem("tokens_in_0"), sem("tokens_in_1")], sem("w_in"), sem("consts"), sem("outs"), sem("passed")
        w12_in, w3_in, w_split = sem("w12_in"), sem("w3_in"), sem("w_split")
        weights_in = 16 * 14

        def sems(n, names):
            return {name: sem(f"{name}_{n}") for name in names.split()}

        both = ("filled emptied stats rstd xn_in hi_in v_hi turned exped p_hi_in p_lo_in pv_done pv_out cx_in cv_back "
                "cp_front ht_in v_done qk_done v_out qk_out spread_done act_spread dve_spread turn_done ")
        of_soft = both + "y_in y_bias scored negm_in masked stats2 rstd2 n2_in cp_back x_in h2_in h2_lo p_lo2_in"
        of_linear = both + "neg_in exp_in full_in"
        phases = [dict(soft=soft, w=0 if soft else 1, back_links=4 if soft else 2,
                       **sems(n, of_soft if soft else of_linear)) for n, soft in enumerate((True, False, True))]
        mixtures = [dict(**sems(f"m{n}", "up_done silu_in hid_in hid_hi_in hid_lo_in down_done added route_in chain e_in"))
                    for n in range(2)]
        for n, ph in enumerate(phases):
            ph["qk_loaded"] = [sem(f"qk_loaded_{n}_{hf}") for hf in range(2)]
            ph["v_loaded"] = [sem(f"v_loaded_{n}_{hf}") for hf in range(2)]
        block = ctx.enter_context(nc.Block())

        def apart(eng):
            eng.sem_inc(passed, 1)

        order = ["b1", "b3", "b6", "b8"]

        def fill_no(ph, b, name):
            per = 4 if ph["soft"] else 2
            return b * per + order.index(name)

        @block.tensor
        def _(pe):
            def fill(ph, b, name):
                if not (isinstance(b, int) and b == 0 and name == "b1"):
                    pe.wait_ge(ph["emptied"], fill_no(ph, b, name))

            def front_turn(ph, b):
                pe.wait_ge(ph["xn_in"], b + 1)
                for t in range(T):
                    ins = nc.tensor.transpose(psum[0][:, t * P:(t + 1) * P], xn[:, t, :], ident[:, :])
                ins.then_inc(ph["turn_done"], 1)

            def front_v(ph, b):
                pe.wait_ge(ph["ht_in"], b + 1)
                if not (isinstance(b, int) and b == 0):
                    pe.wait_ge(ph["v_out"], b)
                for t in range(T):
                    ins = nc.tensor.matmul(psum[1][:, t * P:(t + 1) * P], ht[:, t * P:(t + 1) * P], w_v[ph["w"]][:, :],
                                           start=(t == 0), stop=True, skip_group_check=True)
                ins.then_inc(ph["v_done"], 1)

            def front_qk(ph, b):
                if not (isinstance(b, int) and b == 0):
                    pe.wait_ge(ph["qk_out" if ph["soft"] else "full_in"], b)
                for k in range(2):
                    ins = nc.tensor.matmul(psum[2][:, k * 256:(k + 1) * 256], w_qk[ph["w"]][:, k, :], ht[:, :],
                                           start=(k == 0), stop=True, skip_group_check=True)
                ins.then_inc(ph["qk_done"], 1)

            def front_spread(ph, b, buf):
                pe.wait_ge(ph["qk_out"], b + 1)
                for k in range(2):
                    for g in range(G):
                        n = 2 * k + g // 2
                        if g % 2 == 0 and n in (0, 3) and not (isinstance(b, int) and b == 0):
                            if n == 0:
                                pe.wait_ge(ph["act_spread"], b * 3)
                            else:
                                pe.wait_ge(ph["dve_spread"], b)
                        bank = (psum[3:] + [bank_pv])[n]
                        for part, src in enumerate((qk_hi, qk_lo)):
                            ins = nc.tensor.matmul(bank[:, g % 2 * 256:(g % 2 + 1) * 256],
                                                   sel[:, k, part, g, :, :, :].rearrange("p a b c -> p (a b c)"),
                                                   src[:, buf, k, :], start=(g % 2 == 0 and part == 0),
                                                   stop=(part == 1), skip_group_check=True)
                        if g % 2:
                            ins.then_inc(ph["spread_done"], 1)

            def front_step(ph, b, buf, first=False, last=False):
                front_v(ph, b)
                front_qk(ph, b)
                if not last:
                    front_turn(ph, b + 1)
                if not first:
                    front_spread(ph, b - 1, 1 - buf)

            def front(ph):
                front_turn(ph, 0)
                front_step(ph, 0, 0, first=True)
                with pe.Fori(1, B - 1, 2) as b:
                    front_step(ph, b, 1)
                    front_step(ph, b + 1, 0)
                front_step(ph, B - 1, 1, last=True)
                front_spread(ph, B - 1, 1)
                pe.wait_ge(ph["act_spread"], 3 * B)
                pe.wait_ge(ph["dve_spread"], B)

            def back_turn(ph, b):
                pe.wait_ge(ph["cx_in"], b + 1)
                fill(ph, b, "b1")
                for t in range(T):
                    ins = nc.tensor.transpose(mx[:, t * P:(t + 1) * P], cx[:, t, :], ident[:, :])
                ins.then_inc(ph["filled"], 1)

            def back_wo(ph, b):
                fill(ph, b, "b3")
                for t in range(T):
                    ins = nc.tensor.matmul(mx[:, t * P:(t + 1) * P], cxt[:, t * P:(t + 1) * P], w_o[ph["w"]][:, :],
                                           start=(t == 0), stop=True, skip_group_check=True)
                ins.then_inc(ph["filled"], 1)

            def back_h2(ph, b):
                pe.wait_ge(ph["n2_in"], b + 1)
                fill(ph, b, "b6")
                for t in range(T):
                    ins = nc.tensor.transpose(mx[:, t * P:(t + 1) * P], n2[:, t, :], ident[:, :])
                ins.then_inc(ph["filled"], 1)

            def back_gate(ph, b):
                fill(ph, b, "b8")
                for t in range(T):
                    ins = nc.tensor.matmul(mx[:, t * E:(t + 1) * E], h2t[:, t * P:(t + 1) * P], gw[:, :],
                                           start=(t == 0), stop=True, skip_group_check=True)
                ins.then_inc(ph["filled"], 1)

            def natural(ph, b, g):
                mask = maskb[:, :, :].rearrange("p a b -> p (a b)")
                later = not (isinstance(b, int) and b == 0 and g == 0)
                pe.wait_ge(ph["qk_loaded"][g // 2], LOADS * (b + 1))
                for part, blocks in enumerate((((1, 1, 1), (2, 1, 0)), ((0, 0, 0),))):
                    if later:
                        pe.wait_ge(ph["negm_in"], 2 * (b * S + g) - 1 + part)
                    nc.tensor.matmul(banks_n[:, 1 - part, :], identb[:, :], mask, start=True, stop=False,
                                     skip_group_check=True)
                    for j in range(GH):
                        for c, tq, tk in blocks:
                            ins = nc.tensor.matmul(banks_n[:, c, j * P:(j + 1) * P],
                                                   qst[:, g, j, tq * P:(tq + 1) * P], kst[:, g, tk * P:(tk + 1) * P],
                                                   start=(c == 2 and j == 0), stop=True, skip_group_check=True)
                    ins.then_inc(ph["scored"], 1)

            def turned(ph, b, g):
                if ph["soft"]:
                    pe.wait_ge(ph["negm_in"], 2 * (b * S + g) + 1)
                else:
                    pe.wait_ge(ph["qk_loaded"][g // 2], LOADS * (b + 1))
                banks, free = (banks_t, 1) if ph["soft"] or g % 2 else (banks_n, 2)
                if not ph["soft"]:
                    free = 2
                if not (isinstance(b, int) and b == 0 and g < free):
                    pe.wait_ge(ph["exped"], b * S + g + 1 - free)
                for c, tk, tq in ((1, 1, 1), (2, 0, 1), (0, 0, 0)):
                    if ph["soft"] and c == 0:
                        pe.wait_ge(ph["negm_in"], 2 * (b * S + g) + 2)
                    ins = nc.tensor.matmul(banks[:, c, :], kst[:, g, tk * P:(tk + 1) * P],
                                           qst[:, g, :, tq * P:(tq + 1) * P],
                                           start=True, stop=not ph["soft"], skip_group_check=True)
                    for j in range(GH if ph["soft"] else 0):
                        ins = nc.tensor.matmul(banks_t[:, c, j * P:(j + 1) * P],
                                               negm[:, g % 2, tq, j:j + 1].to_broadcast([P, P]), ident16[:, :],
                                               start=False, stop=True, skip_group_check=True)
                ins.then_inc(ph["turned"], 1)

            def values(ph, b, g):
                pe.wait_ge(ph["v_loaded"][g // 2], 16 * (b + 1))
                pe.wait_ge(ph["p_lo_in"], b * S + g + 1)
                if ph["soft"]:
                    pe.wait_ge(ph["p_lo2_in"], b * S + g + 1)
                if g % 2 == 0 and not (isinstance(b, int) and b == 0 and g == 0):
                    pe.wait_ge(ph["pv_out"], 2 * b + g // 2)
                for j in range(GH):
                    h = GH * g + j
                    for tq, blocks in enumerate((((0, 0),), ((0, 2), (1, 1)))):
                        o = (tq * (H // 2) + h % (H // 2)) * VC
                        todo = [(src, tk, c) for tk, c in blocks for src in parts_of(ph, g)]
                        for i, (src, tk, c) in enumerate(todo):
                            ins = nc.tensor.matmul(bank_pv[:, o:o + VC], src[:, c, j, :],
                                                   v_hl[:, tk, h, :], start=(i == 0), stop=(i == len(todo) - 1),
                                                   skip_group_check=True)
                ins.then_inc(ph["pv_done"], 1)

            def next_natural(ph, b, g, last):
                if ph["soft"] and g + 1 < S:
                    natural(ph, b, g + 1)
                elif ph["soft"] and not last:
                    natural(ph, b + 1, 0)

            def iteration(ph, b, place=2, last=False):
                for g in range(S):
                    next_natural(ph, b, g, last)
                    if ph["soft"] and g == 2 and place > 1:
                        back_h2(ph, b - 2)
                    if g == 3 and place > 0:
                        back_turn(ph, b - 1)
                    turned(ph, b, g)
                    if g < 2 and place > 0:
                        values(ph, b - 1, g + 2)
                    if g >= 2:
                        values(ph, b, g - 2)
                    if ph["soft"] and g == 2 and place > 1:
                        back_gate(ph, b - 2)
                    if g == 3 and place > 0:
                        back_wo(ph, b - 1)

            def attention(ph):
                front(ph)
                if ph["soft"]:
                    natural(ph, 0, 0)
                iteration(ph, 0, place=0)
                iteration(ph, 1, place=1)
                with pe.Fori(2, B - 1) as b:
                    iteration(ph, b)
                iteration(ph, B - 1, last=True)
                values(ph, B - 1, S - 2)
                values(ph, B - 1, S - 1)
                if ph["soft"]:
                    back_h2(ph, B - 2)
                    back_gate(ph, B - 2)
                back_turn(ph, B - 1)
                back_wo(ph, B - 1)
                if ph["soft"]:
                    back_h2(ph, B - 1)
                    back_gate(ph, B - 1)

            def experts(m):
                K = E * HC
                parts = ((0, 0), (0, 1), (1, 0))

                def up(c, k):
                    e, hc = divmod(k, HC)
                    if not (isinstance(c, int) and c == 0 and k < 2):
                        pe.wait_ge(m["hid_in"], c * K + k - 1)
                    for w in range(2):
                        for i, (pw, ph_) in enumerate(parts):
                            ins = nc.tensor.matmul(psum[2 * (k % 2) + w][:, :],
                                                   w12[:, e, w, pw, hc * P:(hc + 1) * P],
                                                   h2t_all[:, ph_, bass.ds(c * CH, CH), :].rearrange("p a b -> p (a b)"),
                                                   start=(i == 0), stop=(i == 2))
                    ins.then_inc(m["up_done"], 1)

                def down(c, k):
                    e, hc = divmod(k, HC)
                    pe.wait_ge(m["hid_lo_in"], c * K + k + 1)
                    if hc == 0 and not (isinstance(c, int) and c == 0 and e < 2):
                        pe.wait_ge(m["added"], c * E + e - 1)
                    for t in range(CH):
                        for i, (phid, pw) in enumerate(parts):
                            ins = nc.tensor.matmul(psum[4 + e % 2][:, t * P:(t + 1) * P],
                                                   (hid_hi, hid_lo)[phid][:, k % 2, t * P:(t + 1) * P],
                                                   w3s[:, pw, e, hc, :],
                                                   start=(hc == 0 and t == 0 and i == 0),
                                                   stop=(hc == HC - 1 and i == 2), skip_group_check=True)
                    ins.then_inc(m["down_done"], 1)

                def chunk(c, first=False):
                    for k in range(K):
                        up(c, k)
                        if k >= 2:
                            down(c, k - 2)
                        elif not first:
                            down(c - 1, K - 2 + k)
                chunk(0, first=True)
                with pe.Fori(1, NT // CH) as c:
                    chunk(c)
                down(NT // CH - 1, K - 2)
                down(NT // CH - 1, K - 1)

            pe.wait_ge(w_in, weights_in)
            pe.wait_ge(consts, 1)
            for n, ph in enumerate(phases):
                attention(ph)
                if ph["soft"]:
                    pe.wait_ge(ph["h2_in"], B)
                    pe.wait_ge(ph["h2_lo"], B)
                    pe.wait_ge(w_split, 4)
                    experts(mixtures[n // 2])

        @block.scalar
        def _(sc):
            def spread_out(ph, b):
                for n, (dst, half_of) in enumerate(((q_all, 0), (q_all, 1), (k_all, 0))):
                    sc.wait_ge(ph["spread_done"], 4 * b + n + 1)
                    nc.scalar.copy(dst[:, b, 2 * half_of:2 * half_of + 2, :].rearrange("p a b -> p (a b)"),
                                   psum[3 + n][:, :]).then_inc(ph["act_spread"], 1)

            def qk_high(ph, b, buf):
                sc.wait_ge(ph["qk_done"], b + 1)
                hi = qk_hi[:, buf, :, :].rearrange("p a b -> p (a b)")
                if ph["soft"]:
                    nc.scalar.copy(hi, psum[2][:, :]).then_inc(ph["hi_in"], 1)
                else:
                    if not (isinstance(b, int) and b == 0):
                        sc.wait_ge(ph["qk_out"], b)
                    nc.scalar.activation(qk_f[:, :, :].rearrange("p a b -> p (a b)"), psum[2][:, :], ACT.Exp)\
                        .then_inc(ph["exp_in"], 1)
                    sc.wait_ge(ph["full_in"], b + 1)
                    nc.scalar.copy(hi, qk_f[:, :, :].rearrange("p a b -> p (a b)")).then_inc(ph["hi_in"], 1)

            def v_high(ph, b):
                sc.wait_ge(ph["v_done"], b + 1)
                nc.scalar.copy(v_all[:, b, :, :, 0:HD], psum[1][:, 0:T * P].rearrange("p (t h d) -> p t h d", t=T, h=H))\
                    .then_inc(ph["v_hi"], 1)

            def front_step(ph, b, buf, first=False):
                v_high(ph, b)
                qk_high(ph, b, buf)
                if not first:
                    spread_out(ph, b - 1)

            def front(ph):
                front_step(ph, 0, 0, first=True)
                with sc.Fori(1, B - 1, 2) as b:
                    front_step(ph, b, 1)
                    front_step(ph, b + 1, 0)
                front_step(ph, B - 1, 1)
                spread_out(ph, B - 1)

            def exps(ph, b, g):
                sc.wait_ge(ph["turned"], b * S + g + 1)
                flat = "p a b c -> p (a b c)"
                if ph["soft"]:
                    if not (isinstance(b, int) and b == 0 and g < 2):
                        sc.wait_ge(ph["p_lo_in"], b * S + g - 1)
                        sc.wait_ge(ph["p_lo2_in"], b * S + g - 1)
                    nc.scalar.activation(pf[:, g % 2, :, :, :].rearrange(flat),
                                         banks_t[:, :, :].rearrange("p a b -> p (a b)"), ACT.Exp,
                                         scale=HD ** -0.5).then_inc(ph["exped"], 1)
                else:
                    if not (isinstance(b, int) and b == 0):
                        sc.wait_ge(ph["pv_done"], b * S + g + 1 - 4)
                    nc.scalar.copy(parts_of(ph, g)[0].rearrange(flat),
                                   (banks_t if g % 2 else banks_n)[:, :, :].rearrange("p a b -> p (a b)")).then_inc(ph["p_hi_in"], 1)

            def p_high(ph, b, g):
                if not ph["soft"]:
                    return
                sc.wait_ge(ph["masked"], b * S + g + 1)
                if not (isinstance(b, int) and b == 0 and g < 2):
                    sc.wait_ge(ph["pv_done"], b * S + g - 1)
                flat = "p a b c -> p (a b c)"
                nc.scalar.copy(p_hi[:, g % 2, :, :, :].rearrange(flat), pf[:, g % 2, :, :, :].rearrange(flat))\
                    .then_inc(ph["p_hi_in"], 1)

            def pv_read(ph, b, hf):
                sc.wait_ge(ph["pv_done"], b * S + 2 * (hf + 1))
                nc.scalar.copy(pv_sb[:, :, hf * 8:(hf + 1) * 8, :],
                               bank_pv[:, 0:T * 8 * VC].rearrange("p (t h d) -> p t h d", t=T, h=8))\
                    .then_inc(ph["pv_out"], 1)

            def ctx_turned(ph, b):
                sc.wait_ge(ph["filled"], fill_no(ph, b, "b1") + 1)
                nc.scalar.copy(cxt[:, :], mx[:, 0:T * P]).then_inc(ph["emptied"], 1)

            def h2_turned(ph, b):
                sc.wait_ge(ph["filled"], fill_no(ph, b, "b6") + 1)
                if not (isinstance(b, int) and b == 0):
                    sc.wait_ge(ph["h2_lo"], b)
                nc.scalar.activation(h2t[:, :], mx[:, 0:T * P], ACT.Identity,
                                     scale=ln[:, 2:3], bias=ln[:, 3:4]).then_inc(ph["h2_in"], 1)
                nc.scalar.activation(h2t_all[:, 0, bass.ds(2 * b, 2), :].rearrange("p a b -> p (a b)"),
                                     mx[:, 0:T * P], ACT.Identity, scale=ln[:, 2:3], bias=ln[:, 3:4])\
                    .then_inc(ph["emptied"], 1)

            def gates_out(ph, b):
                sc.wait_ge(ph["filled"], fill_no(ph, b, "b8") + 1)
                nc.scalar.copy(gates[:, bass.ds(2 * b, 2), :].rearrange("p a b -> p (a b)"), mx[:, 0:T * E])\
                    .then_inc(ph["emptied"], 1)

            def iteration(ph, b, place=2, last=False):
                for g in range(S):
                    if ph["soft"] and g == 2 and place > 1:
                        h2_turned(ph, b - 2)
                    if ph["soft"] and g == 3 and place > 1:
                        gates_out(ph, b - 2)
                    if g == 3 and place > 0:
                        ctx_turned(ph, b - 1)
                    if g:
                        p_high(ph, b, g - 1)
                    elif place > 0:
                        p_high(ph, b - 1, S - 1)
                    exps(ph, b, g)
                    if g == 1 and place > 0:
                        pv_read(ph, b - 1, 1)
                    if g == 3:
                        pv_read(ph, b, 0)

            def attention(ph):
                front(ph)
                iteration(ph, 0, place=0)
                iteration(ph, 1, place=1)
                with sc.Fori(2, B) as b:
                    iteration(ph, b)
                p_high(ph, B - 1, S - 1)
                if ph["soft"]:
                    h2_turned(ph, B - 2)
                    gates_out(ph, B - 2)
                pv_read(ph, B - 1, 1)
                ctx_turned(ph, B - 1)
                if ph["soft"]:
                    h2_turned(ph, B - 1)
                    gates_out(ph, B - 1)

            def experts(m):
                K = E * HC

                def chunk(c, first=False):
                    for k in range(K):
                        sc.wait_ge(m["up_done"], c * K + k + 1)
                        if not (first and k < 2):
                            sc.wait_ge(m["hid_in"], c * K + k - 1)
                        nc.scalar.activation(act_s[:, k % 2, :], psum[2 * (k % 2)][:, :], ACT.Silu)\
                            .then_inc(m["silu_in"], 1)
                        sc.wait_ge(m["hid_in"], c * K + k + 1)
                        if not (first and k < 2):
                            sc.wait_ge(m["down_done"], c * K + k - 1)
                        nc.scalar.copy(hid_hi[:, k % 2, :], hid[:, k % 2, :]).then_inc(m["hid_hi_in"], 1)
                        if first and k == 3:
                            sc.wait_ge(m["route_in"], 1)
                            nc.scalar.activation(prob[:, :, 0], prob[:, :, 0], ACT.Exp).then_inc(m["e_in"], 1)
                chunk(0, first=True)
                with sc.Fori(1, NT // CH) as c:
                    chunk(c)

            sc.wait_ge(w_in, weights_in)
            for n, ph in enumerate(phases):
                attention(ph)
                if ph["soft"]:
                    experts(mixtures[n // 2])

        @block.vector
        def _(ve):
            def front_stats(ph, part):
                for n in STATS[part]:
                    ins = nc.vector.bn_stats(st[:, n, :], x_all[:, n // T, n % T, :])
                ins.then_inc(ph["stats"], 1)
                ve.wait_ge(ph["stats"], 2 * part + 1)
                for n in STATS[part]:
                    ins = nc.vector.bn_aggr(mv[:, n, :], st[:, n, :])
                ins.then_inc(ph["stats"], 1)

            def front_norm(ph, b):
                def of(array, t):
                    return array[:, bass.ds(T * b + t, 1)]
                for t in range(T):
                    ins = nc.vector.tensor_scalar(xn[:, t, :], x_all[:, b, t, :], of(mv[:, :, 0], t),
                                                  of(rs[:, 5 if ph["soft"] else 1, :], t), ALU.subtract, ALU.mult)
                ins.then_inc(ph["xn_in"], 1)

            def back_y(ph, b):
                def of(array, t):
                    return array[:, bass.ds(T * b + t, 1)]
                for t in range(T):
                    ins = nc.vector.tensor_scalar(yb[:, t, :], x_all[:, b, t, :], of(mv[:, :, 0], t),
                                                  of(rs[:, 1, :], t), ALU.subtract, ALU.mult)
                ins.then_inc(ph["y_in"], 1)

            def front_ht(ph, b):
                ve.wait_ge(ph["turn_done"], b + 1)
                if ph["soft"]:
                    nc.vector.tensor_scalar(ht[:, :], psum[0][:, 0:T * P], ln[:, 0:1], ln[:, 1:2], ALU.mult, ALU.add)\
                        .then_inc(ph["ht_in"], 1)
                else:
                    nc.vector.tensor_copy(ht[:, :], psum[0][:, 0:T * P]).then_inc(ph["ht_in"], 1)

            def qk_elu(ph, b):
                if ph["soft"]:
                    return
                flat = qk_f[:, :, :].rearrange("p a b -> p (a b)")
                ve.wait_ge(ph["exp_in"], b + 1)
                nc.vector.tensor_scalar(flat, flat, 1.0, None, ALU.min).then_inc(ph["neg_in"], 1)
                ve.wait_ge(ph["neg_in"], b + 1)
                nc.vector.scalar_tensor_tensor(flat, psum[2][:, :], 0.0, flat, ALU.max, ALU.add)\
                    .then_inc(ph["full_in"], 1)

            def qk_low(ph, b, buf):
                ve.wait_ge(ph["hi_in"], b + 1)
                nc.vector.tensor_tensor(qk_lo[:, buf, :, :].rearrange("p a b -> p (a b)"),
                                        psum[2][:, :] if ph["soft"] else qk_f[:, :, :].rearrange("p a b -> p (a b)"),
                                        qk_hi[:, buf, :, :].rearrange("p a b -> p (a b)"), ALU.subtract)\
                    .then_inc(ph["qk_out"], 1)

            def spread_out(ph, b):
                ve.wait_ge(ph["spread_done"], 4 * b + 4)
                nc.vector.tensor_copy(k_all[:, b, 2:4, :].rearrange("p a b -> p (a b)"), bank_pv[:, :])\
                    .then_inc(ph["dve_spread"], 1)

            def v_low(ph, b):
                ve.wait_ge(ph["v_hi"], b + 1)
                nc.vector.tensor_tensor(v_all[:, b, :, :, HD + 1:VC],
                                        psum[1][:, 0:T * P].rearrange("p (t h d) -> p t h d", t=T, h=H),
                                        v_all[:, b, :, :, 0:HD], ALU.subtract).then_inc(ph["v_out"], 1)

            def front_step(ph, b, buf, first=False, last=False, before_last=False):
                v_low(ph, b)
                if not last:
                    front_ht(ph, b + 1)
                if not (last or before_last):
                    front_norm(ph, b + 2)
                qk_elu(ph, b)
                qk_low(ph, b, buf)
                if not first:
                    spread_out(ph, b - 1)

            def front(ph):
                if ph is phases[0]:
                    ve.wait_ge(x_in[0], 16)
                front_stats(ph, 0)
                if ph is phases[0]:
                    ve.wait_ge(x_in[1], 16)
                front_stats(ph, 1)
                ve.wait_ge(ph["rstd"], 1)
                front_norm(ph, 0)
                front_ht(ph, 0)
                front_norm(ph, 1)
                front_step(ph, 0, 0, first=True)
                front_stats(ph, 2)
                ve.wait_ge(ph["rstd"], 2)
                for start, end in ((1, 5), (5, B - 3)):
                    if start > 1:
                        ve.wait_ge(ph["rstd"], 3)
                    with ve.Fori(start, end, 2) as b:
                        front_step(ph, b, 1)
                        front_step(ph, b + 1, 0)
                front_step(ph, B - 3, 1)
                front_step(ph, B - 2, 0, before_last=True)
                front_step(ph, B - 1, 1, last=True)
                spread_out(ph, B - 1)

            def maxima(ph, b, g):
                if not ph["soft"]:
                    return
                ve.wait_ge(ph["scored"], 2 * (b * S + g) + 1)
                nc.vector.tensor_reduce(negm[:, g % 2, 1, :],
                                        banks_n[:, 1:3, :].rearrange("p c (h k) -> p h c k", h=GH),
                                        AX.XY, ALU.max, negate=True).then_inc(ph["negm_in"], 1)
                ve.wait_ge(ph["scored"], 2 * (b * S + g) + 2)
                nc.vector.tensor_reduce(negm[:, g % 2, 0, :], banks_n[:, 0, :].rearrange("p (h k) -> p h k", h=GH),
                                        AX.X, ALU.max, negate=True).then_inc(ph["negm_in"], 1)

            def p_low(ph, b, g):
                ve.wait_ge(ph["p_hi_in"], b * S + g + 1)
                flat = "p a b c -> p (a b c)"
                hi, lo = [a.rearrange(flat) for a in parts_of(ph, g)]
                if ph["soft"]:
                    two = slice(0, 2 * GH * P)
                    nc.vector.tensor_tensor(lo[:, two], pf[:, g % 2, :, :, :].rearrange(flat)[:, two], hi[:, two],
                                            ALU.subtract)\
                        .then_inc(ph["p_lo_in"], 1)
                else:
                    nc.vector.tensor_tensor(lo, (banks_t if g % 2 else banks_n)[:, :, :].rearrange("p a b -> p (a b)"), hi, ALU.subtract)\
                        .then_inc(ph["exped"], 1)

            def back_context(ph, b):
                c = Chain(ve, ph["cv_back"], b * ph["back_links"])
                ve.wait_ge(ph["pv_out"], 2 * b + 2)
                if ph["soft"]:
                    c.link(nc.vector.tensor_tensor(num[:, :, :, :], pv_sb[:, :, :, 0:HD], pv_sb[:, :, :, HD + 1:VC],
                                                   ALU.add))
                    c.link(nc.vector.reciprocal(rden[:, :, :], pv_sb[:, :, :, HD]))
                else:
                    c.link(nc.vector.tensor_scalar(rden[:, :, :], pv_sb[:, :, :, HD], 1e-6, None, ALU.max))
                    nc.vector.tensor_tensor(num[:, :, :, :], pv_sb[:, :, :, 0:HD], pv_sb[:, :, :, HD + 1:VC], ALU.add)
                    c.link(nc.vector.reciprocal(rden[:, :, :], rden[:, :, :]))
                nc.vector.tensor_tensor(cx[:, :, :].rearrange("p t (h d) -> p t h d", h=H), num[:, :, :, :],
                                        rden[:, :, :].unsqueeze(3).to_broadcast([P, T, H, HD]), ALU.mult)\
                    .then_inc(ph["cx_in"], 1)

            def back_add(ph, b):
                ve.wait_ge(ph["filled"], fill_no(ph, b, "b3") + 1)
                src = mx[:, 0:T * P].rearrange("p (t d) -> p t d", t=T)
                if not ph["soft"]:
                    nc.vector.tensor_tensor(x_all[:, b, :, :], src, x_all[:, b, :, :], ALU.add)\
                        .then_inc(ph["emptied"], 1)
                    return
                c = Chain(ve, ph["cv_back"], b * ph["back_links"])
                c.n = 2
                ve.wait_ge(ph["y_bias"], b + 1)
                nc.vector.tensor_tensor(y2[:, :, :], src, yb[:, :, :], ALU.add).then_inc(ph["emptied"], 1)
                ve.wait_ge(ph["emptied"], fill_no(ph, b, "b3") + 1)
                for t in range(T):
                    c.link(nc.vector.bn_stats(st2[:, t, :], y2[:, t, :]))
                apart(ve)
                nc.vector.bn_aggr(mv2[:, 0, :], st2[:, 0, :])
                nc.vector.bn_aggr(mv2[:, 1, :], st2[:, 1, :]).then_inc(ph["stats2"], 1)
                c.end(ph["back_links"])

            def back_norm(ph, b):
                ve.wait_ge(ph["rstd2"], b + 1)
                for t in range(T):
                    ins = nc.vector.tensor_scalar(n2[:, t, :], y2[:, t, :], mv2[:, t, 0:1],
                                                  rs2[:, 1, t:t + 1], ALU.subtract, ALU.mult)
                ins.then_inc(ph["n2_in"], 1)
                nc.vector.scalar_tensor_tensor(x_all[:, b, :, :], y2[:, :, :], 0.5, x_all[:, b, :, :],
                                               ALU.mult, ALU.add).then_inc(ph["x_in"], 1)

            def iteration(ph, b, place=2, last=False):
                for g in range(S):
                    if g + 1 < S:
                        maxima(ph, b, g + 1)
                    elif not last:
                        maxima(ph, b + 1, 0)
                    if g == 0 and place > 1:
                        back_add(ph, b - 2)
                    if ph["soft"] and g == 1 and place > 1:
                        back_norm(ph, b - 2)
                    if ph["soft"] and g == 3 and place > 0:
                        back_y(ph, b - 1)
                    if g == 2 and place > 0:
                        back_context(ph, b - 1)
                    if not ph["soft"]:
                        p_low(ph, b, g)
                    elif g:
                        p_low(ph, b, g - 1)
                    elif place > 0:
                        p_low(ph, b - 1, S - 1)

            def attention(ph):
                front(ph)
                maxima(ph, 0, 0)
                iteration(ph, 0, place=0)
                iteration(ph, 1, place=1)
                with ve.Fori(2, B - 1) as b:
                    iteration(ph, b)
                iteration(ph, B - 1, last=True)
                if ph["soft"]:
                    p_low(ph, B - 1, S - 1)
                back_add(ph, B - 2)
                if ph["soft"]:
                    back_norm(ph, B - 2)
                    back_y(ph, B - 1)
                back_context(ph, B - 1)
                back_add(ph, B - 1)
                if ph["soft"]:
                    back_norm(ph, B - 1)

            def experts(ph, m):
                K = E * HC

                def routing():
                    c = Chain(ve, m["chain"], 0)
                    ve.wait_ge(ph["emptied"], fill_no(ph, B - 1, "b8") + 1)
                    ve.wait_ge(ph["x_in"], B)
                    for n in range(NT):
                        ins = nc.vector.max(top[:, n, :], gates[:, n, :])
                    c.link(ins)
                    for n in range(NT):
                        ins = nc.vector.max_index(topi[:, n, :], top[:, n, :], gates[:, n, :])
                    nc.vector.tensor_tensor(prob[:, :, 0], top[:, :, 1], top[:, :, 0], ALU.subtract)\
                        .then_inc(m["route_in"], 1)
                    c.link(ins)
                    c.link(nc.vector.tensor_copy(topf[:, :, :], topi[:, :, 0:2]))
                    ve.wait_ge(m["e_in"], 1)
                    c.link(nc.vector.tensor_scalar(prob[:, :, 1], prob[:, :, 0], 1.0, None, ALU.add))
                    c.link(nc.vector.reciprocal(prob[:, :, 1], prob[:, :, 1]))
                    c.link(nc.vector.tensor_scalar(prob[:, :, 1], prob[:, :, 1], 0.5, None, ALU.mult))
                    c.link(nc.vector.tensor_tensor(prob[:, :, 2], prob[:, :, 0], prob[:, :, 1], ALU.mult))
                    for k, dst in ((0, route), (1, onehot)):
                        c.link(nc.vector.tensor_tensor(dst[:, :, :], iota_e[:, :].unsqueeze(1).to_broadcast([P, NT, E]),
                                                       topf[:, :, k:k + 1].to_broadcast([P, NT, E]), ALU.is_equal))
                        c.link(nc.vector.tensor_tensor(dst[:, :, :], dst[:, :, :],
                                                       prob[:, :, k + 1:k + 2].to_broadcast([P, NT, E]), ALU.mult))
                    c.link(nc.vector.tensor_tensor(route[:, :, :], route[:, :, :], onehot[:, :, :], ALU.add))

                def product(cc, k):
                    ve.wait_ge(m["silu_in"], cc * K + k + 1)
                    if not (isinstance(cc, int) and cc == 0 and k < 2):
                        ve.wait_ge(m["hid_lo_in"], cc * K + k - 1)
                    nc.vector.tensor_tensor(hid[:, k % 2, :], psum[2 * (k % 2) + 1][:, :], act_s[:, k % 2, :],
                                            ALU.mult).then_inc(m["hid_in"], 1)

                def add(cc, e):
                    ve.wait_ge(m["down_done"], cc * K + HC * (e + 1))
                    if not (isinstance(cc, int) and cc == 0 and e == 0):
                        ve.wait_ge(m["added"], cc * E + e)
                    for t in range(CH):
                        y = x_all[:, :, :, :].rearrange("p b t d -> p (b t) d")[:, bass.ds(cc * CH + t, 1), :]\
                            .rearrange("p a d -> p (a d)")
                        r = route[:, bass.ds(cc * CH + t, 1), e:e + 1].rearrange("p a b -> p (a b)")
                        ins = nc.vector.scalar_tensor_tensor(y, psum[4 + e % 2][:, t * P:(t + 1) * P], r, y,
                                                             ALU.mult, ALU.add)
                    ins.then_inc(m["added"], 1)

                def chunk(cc, first=False):
                    for k in range(K):
                        product(cc, k)
                        if first and k == 3:
                            routing()
                        if k >= 4 and k % 2 == 0:
                            add(cc, k // 2 - 2)
                        if k in (0, 2) and not first:
                            add(cc - 1, E - 2 + k // 2)
                chunk(0, first=True)
                with ve.Fori(1, NT // CH) as cc:
                    chunk(cc)
                add(NT // CH - 1, E - 2)
                add(NT // CH - 1, E - 1)
                ve.wait_ge(m["added"], NT // CH * E)

            ve.wait_ge(w_in, weights_in)
            ve.wait_ge(consts, 1)
            for n, ph in enumerate(phases):
                attention(ph)
                if not ph["soft"]:
                    ve.wait_ge(ph["emptied"], fill_no(ph, B - 1, "b3") + 1)
                if ph["soft"]:
                    experts(ph, mixtures[n // 2])

        @block.gpsimd
        def _(gp):
            pools = sem("pools")
            c = Chain(gp, pools, 0)

            def diag(t, fill=1.0):
                c.link(nc.gpsimd.memset(t, 0.0))
                c.link(nc.gpsimd.affine_select(out=t, in_=t, pattern=[[-1, P]], compare_op=ALU.not_equal, fill=fill,
                                               base=0, channel_multiplier=1))
            diag(ident[:, :])
            diag(ident16[:, :])
            diag(identb[:, :])
            c.link(nc.gpsimd.memset(maskb[:, :, :], 0.0))
            c.link(nc.gpsimd.affine_select(out=maskb[:, :, :], in_=maskb[:, :, :], pattern=[[0, GH], [-1, P]],
                                           compare_op=ALU.is_ge, fill=BIG, base=0, channel_multiplier=1))
            c.link(nc.gpsimd.memset(sel[:, :, :, :, :, :, :], 0.0))
            for k, rows in enumerate((((0, 1), (2,)), ((0, 2), (1,)))):
                for part, blocks in enumerate(rows):
                    for r in blocks:
                        at = sel[:, k, part, :, :, r, :]
                        c.link(nc.gpsimd.affine_select(out=at, in_=at, pattern=[[-32, G], [-8, 4], [-1, HD]],
                                                       compare_op=ALU.not_equal, fill=1.0, base=0,
                                                       channel_multiplier=1))
            c.link(nc.gpsimd.memset(v_all[:, :, :, :, HD:HD + 1].rearrange("p a b c d -> p (a b c) d"), 1.0))
            c.link(nc.gpsimd.memset(qst[:, :, :, :].rearrange("p a b c -> p (a b c)"), 0.0))
            c.link(nc.gpsimd.memset(half[:, :], -0.5))
            nc.gpsimd.iota(iota_e[:, :], pattern=[[1, E]], base=0, channel_multiplier=0,
                           allow_small_or_imprecise_dtypes=True).then_inc(consts, 1)

            def split_weights():
                flat = "p e w h -> p (e w) h"
                gp.wait_ge(w12_in, 16 * 4)
                c = Chain(gp, w_split, 0)
                c.link(nc.gpsimd.tensor_scalar(w12[:, :, :, 0, :].rearrange(flat), stage12.rearrange(flat), 1.0, None,
                                               ALU.mult))
                c.link(nc.gpsimd.tensor_tensor(w12[:, :, :, 1, :].rearrange(flat), stage12.rearrange(flat),
                                               w12[:, :, :, 0, :].rearrange(flat), ALU.subtract))
                gp.wait_ge(w3_in, 16 * 4)
                c.link(nc.gpsimd.tensor_scalar(w3s[:, 0, :, :, :].rearrange(flat), stage3.rearrange(flat), 1.0, None,
                                               ALU.mult))
                c.link(nc.gpsimd.tensor_tensor(w3s[:, 1, :, :, :].rearrange(flat), stage3.rearrange(flat),
                                               w3s[:, 0, :, :, :].rearrange(flat), ALU.subtract))

            def h2_low(ph, b):
                gp.wait_ge(ph["emptied"], fill_no(ph, b, "b6") + 1)
                apart(gp)
                two = bass.ds(2 * b, 2)
                flat = "p a b -> p (a b)"
                nc.gpsimd.tensor_tensor(h2t_all[:, 1, two, :].rearrange(flat), h2t[:, :],
                                        h2t_all[:, 0, two, :].rearrange(flat), ALU.subtract).then_inc(ph["h2_lo"], 1)

            def front_rstd(ph, part):
                s = slice(STATS[part][0], STATS[part][-1] + 1)
                c = Chain(gp, ph["cp_front"], part * (6 if ph["soft"] else 1))
                gp.wait_ge(ph["stats"], 2 * part + 2)
                c.link(nc.gpsimd.tensor_scalar(rs[:, 0, s], mv[:, s, 1], EPS, None, ALU.add))
                if not ph["soft"]:
                    nc.gpsimd.tensor_tensor(rs[:, 1, s], rs[:, 0, s], half[:, s], ALU.pow).then_inc(ph["rstd"], 1)
                    return
                c.link(nc.gpsimd.tensor_tensor(rs[:, 1, s], rs[:, 0, s], half[:, s], ALU.pow))
                c.link(nc.gpsimd.tensor_tensor(rs[:, 2, s], mv[:, s, 1], rs[:, 1, s], ALU.mult))
                c.link(nc.gpsimd.tensor_tensor(rs[:, 2, s], rs[:, 2, s], rs[:, 1, s], ALU.mult))
                c.link(nc.gpsimd.tensor_scalar(rs[:, 3, s], rs[:, 2, s], EPS, None, ALU.add))
                c.link(nc.gpsimd.tensor_tensor(rs[:, 4, s], rs[:, 3, s], half[:, s], ALU.pow))
                nc.gpsimd.tensor_tensor(rs[:, 5, s], rs[:, 4, s], rs[:, 1, s], ALU.mult).then_inc(ph["rstd"], 1)

            def back_bias(ph, b):
                gp.wait_ge(ph["y_in"], b + 1)
                nc.gpsimd.tensor_tensor(yb[:, :, :], yb[:, :, :], bo_b[:, :].unsqueeze(1).to_broadcast([P, T, P]),
                                        ALU.add).then_inc(ph["y_bias"], 1)

            def back_rstd(ph, b):
                c = Chain(gp, ph["cp_back"], b)
                gp.wait_ge(ph["stats2"], b + 1)
                apart(gp)
                c.link(nc.gpsimd.tensor_scalar(rs2[:, 0, :], mv2[:, :, 1], EPS, None, ALU.add))
                nc.gpsimd.tensor_tensor(rs2[:, 1, :], rs2[:, 0, :], half[:, 0:T], ALU.pow).then_inc(ph["rstd2"], 1)

            def causal(ph, b, g):
                def select(src):
                    at = src[:, 0:2, :, :].rearrange("p a b c -> p (a b c)")
                    return nc.gpsimd.affine_select(out=at, in_=at, pattern=[[0, 2 * GH], [1, P]],
                                                   compare_op=ALU.is_ge, fill=0.0, base=0, channel_multiplier=-1)
                gp.wait_ge(ph["exped"], b * S + g + 1)
                apart(gp)
                if ph["soft"]:
                    select(pf[:, g % 2, :, :, :]).then_inc(ph["masked"], 1)
                else:
                    hi, lo = parts_of(ph, g)
                    select(hi)
                    select(lo).then_inc(ph["p_lo_in"], 1)

            def p_low(ph, b, g):
                gp.wait_ge(ph["p_hi_in"], b * S + g + 1)
                flat = "p b c -> p (b c)"
                nc.gpsimd.tensor_tensor(p_lo[:, g % 2, 2, :, :].rearrange(flat), pf[:, g % 2, 2, :, :].rearrange(flat),
                                        p_hi[:, g % 2, 2, :, :].rearrange(flat), ALU.subtract)\
                    .then_inc(ph["p_lo2_in"], 1)

            def iteration(ph, b, place=2):
                for g in range(S):
                    causal(ph, b, g)
                    if ph["soft"] and g:
                        p_low(ph, b, g - 1)
                    elif ph["soft"] and place > 0:
                        p_low(ph, b - 1, S - 1)
                    if ph["soft"] and g == 0 and place > 1:
                        back_rstd(ph, b - 2)
                    if ph["soft"] and g == 3 and place > 0:
                        back_bias(ph, b - 1)
                    if ph["soft"] and g == 2 and place > 1:
                        h2_low(ph, b - 2)

            def experts(m):
                K = E * HC

                def chunk(cc, first=False):
                    for k in range(K):
                        gp.wait_ge(m["hid_hi_in"], cc * K + k + 1)
                        if not (first and k < 2):
                            gp.wait_ge(m["down_done"], cc * K + k - 1)
                        nc.gpsimd.tensor_tensor(hid_lo[:, k % 2, :], hid[:, k % 2, :], hid_hi[:, k % 2, :],
                                                ALU.subtract).then_inc(m["hid_lo_in"], 1)
                chunk(0, first=True)
                with gp.Fori(1, NT // CH) as cc:
                    chunk(cc)

            def attention(ph):
                for part in range(3):
                    front_rstd(ph, part)
                if ph is phases[0]:
                    split_weights()
                iteration(ph, 0, place=0)
                iteration(ph, 1, place=1)
                with gp.Fori(2, B) as b:
                    iteration(ph, b)
                if ph["soft"]:
                    p_low(ph, B - 1, S - 1)
                    back_rstd(ph, B - 2)
                    back_bias(ph, B - 1)
                    h2_low(ph, B - 2)
                    back_rstd(ph, B - 1)
                    h2_low(ph, B - 1)

            gp.wait_ge(w_in, weights_in)
            for n, ph in enumerate(phases):
                attention(ph)
                if ph["soft"]:
                    experts(mixtures[n // 2])

        @block.sync
        def _(sy):
            def load_tokens(n, bs):
                sy.dma_start(x_all[:, bs, :, :], x.rearrange("b (t p) d -> p b t d", p=P)[:, bs]).then_inc(x_in[n], 16)

            load_tokens(0, slice(0, STATS[0][-1] // T + 1))
            n = 0
            for k, (q_, k_, v_, o_) in enumerate(((wq, wk, wv, wo), (Wq, Wk, Wv, Wo))):
                for dst, src in ((w_qk[k][:, 0, :], q_), (w_qk[k][:, 1, :], k_), (w_v[k][:, :], v_), (w_o[k][:, :], o_)):
                    sy.dma_start(dst, src).then_inc(w_in, 16)
                    n += 1
            for k, src in enumerate((ln1_s, ln1_b, ln2_s, ln2_b)):
                sy.dma_start(ln[:, k:k + 1], src.rearrange("(p a) -> p a", a=1)).then_inc(w_in, 16)
                n += 1
            sy.dma_start(bo_b[:, :], bo.unsqueeze(0).to_broadcast([P, P])).then_inc(w_in, 16)
            sy.dma_start(gw[:, :], gate_w).then_inc(w_in, 16)
            n += 2
            assert n * 16 == weights_in, n
            load_tokens(1, slice(STATS[0][-1] // T + 1, B))
            for e0 in (0, 4):
                for k, src in enumerate((w1, w2)):
                    sy.dma_start(stage12[:, e0:e0 + 4, k, :], src[e0:e0 + 4].rearrange("e d h -> d e h"))\
                        .then_inc(w12_in, 16)
            sy.wait_ge(w_split, 2)
            for c in range(HC):
                for e0 in (0, 4):
                    sy.dma_start(stage3[:, e0:e0 + 4, c, :],
                                 w3[e0:e0 + 4, c * P:(c + 1) * P, :].rearrange("e h d -> h e d")).then_inc(w3_in, 16)

            def load_qk(ph, b, hf):
                gs = slice(2 * hf, 2 * hf + 2)
                for j in range(GH):
                    rows = slice(32 * j, 32 * (j + 1))
                    sy.dma_start(qst[rows, gs, j, :], q_all[rows, b, gs, :]).then_inc(ph["qk_loaded"][hf], 16)
                sy.dma_start(kst[:, gs, :], k_all[:, b, gs, :]).then_inc(ph["qk_loaded"][hf], 16)

            def load_v(ph, b, hf):
                heads = slice(8 * hf, 8 * (hf + 1))
                sy.dma_start(v_hl[:, :, heads, :], v_all[:, b, :, heads, :]).then_inc(ph["v_loaded"][hf], 16)

            def next_v(ph, b, hf):
                sy.wait_ge(ph["pv_done"], b * S + 2 * hf + 2)
                load_v(ph, b + 1, hf)

            def next_qk(ph, b, hf):
                sy.wait_ge(ph["turned"], b * S + 2 * hf + 2)
                load_qk(ph, b + 1, hf)

            def attention(ph):
                sy.wait_ge(ph["act_spread"], 3)
                sy.wait_ge(ph["dve_spread"], 1)
                sy.wait_ge(ph["v_out"], 1)
                for hf in range(2):
                    load_qk(ph, 0, hf)
                for hf in range(2):
                    load_v(ph, 0, hf)
                sy.wait_ge(ph["act_spread"], 3 * B)
                sy.wait_ge(ph["dve_spread"], B)
                sy.wait_ge(ph["v_out"], B)
                next_qk(ph, 0, 0)
                next_qk(ph, 0, 1)
                next_v(ph, 0, 0)
                with sy.Fori(1, B - 1) as b:
                    next_qk(ph, b, 0)
                    next_v(ph, b - 1, 1)
                    next_qk(ph, b, 1)
                    next_v(ph, b, 0)
                next_v(ph, B - 2, 1)

            sy.wait_ge(consts, 1)
            for ph in phases:
                attention(ph)
            sy.wait_ge(mixtures[1]["added"], NT // CH * E)
            sy.dma_start(out.rearrange("b (t p) d -> p b t d", p=P), x_all[:, :, :, :]).then_inc(outs, 16)
            sy.wait_ge(outs, 16)


_INS = ["L0_attn_x", "L0_attn_Wq", "L0_attn_Wk", "L0_attn_Wv", "L0_attn_Wo", "L0_ffn_ln1_scale", "L0_ffn_ln1_shift",
        "L0_ffn_wq", "L0_ffn_wk", "L0_ffn_wv", "L0_ffn_wo", "L0_ffn_bo", "L0_ffn_ln2_scale", "L0_ffn_ln2_shift",
        "L0_ffn_gate_w", "L0_ffn_w1", "L0_ffn_w2", "L0_ffn_w3"]


def kernel(**inputs):
    import numpy as np
    import concourse.bacc as bacc
    from concourse.bass_utils import run_bass_kernel_spmd

    nc = bacc.Bacc("TRN2", target_bir_lowering=False, num_devices=1)
    arrays, args = {}, []
    for name in _INS:
        a = np.asarray(inputs[name])
        if name.startswith("L0_attn_W"):
            a = a.T
        arrays[name] = np.ascontiguousarray(a)
        args.append(nc.dram_tensor(name, a.shape, F32, kind="ExternalInput").ap())
    args.append(nc.dram_tensor("out", inputs["L0_attn_x"].shape, F32, kind="ExternalOutput").ap())
    build(nc, *args)
    return run_bass_kernel_spmd(nc, [arrays], core_ids=[0]).results[0]["out"]
```
